# Optimizing a Trainium2 kernel written in Bass

```python
import numpy as np
import jax
import jax.numpy as jnp

def _softmax(x, axis=-1):
    return jax.nn.softmax(x, axis=axis)

def _gelu(x):
    return jax.nn.gelu(x, approximate=True)

def _silu(x):
    return jax.nn.silu(x)

def _sigmoid(x):
    return jax.nn.sigmoid(x)

def _layernorm(x, axis=-1, eps=1e-05):
    m = jnp.mean(x, axis=axis, keepdims=True)
    v = jnp.var(x, axis=axis, keepdims=True)
    return (x - m) / jnp.sqrt(v + eps)

def _scatter_add(tgt, idx, src, axis=0):
    return tgt.at[idx].add(src)

def _segment_sum(src, seg, n):
    return jax.ops.segment_sum(src, seg, n)
kernel_name = 'mk_gnn_preln_d1_gnn_r8_569a99'

def setup_inputs(seed: int=0):
    np.random.seed(seed)
    _w = jnp.asarray

    def _rec_inputs():
        import jax
        import jax.numpy as jnp
        _gk = jax.random.key(seed)
        x = -0.0001006 + 1 * jax.random.normal(jax.random.fold_in(_gk, 1), (6250, 96), jnp.float32)
        _s = jax.random.randint(jax.random.fold_in(_gk, 2), (50000,), 0, 6250, jnp.int32)
        _d = jax.random.randint(jax.random.fold_in(_gk, 3), (50000,), 0, 6250, jnp.int32)
        _loop = jnp.arange(6250, dtype=jnp.int32)
        src = jnp.concatenate([_s, _d, _loop])
        dst = jnp.concatenate([_d, _s, _loop])
        _o = jnp.argsort(dst, stable=True)
        src = src[_o]
        dst = dst[_o]
        edge_attr_96 = 5.93493e-05 + 1.00006 * jax.random.normal(jax.random.fold_in(_gk, 11), (106250, 96), jnp.float32)
        return (x, src, dst, edge_attr_96)
    x, src, dst, edge_attr_96 = _rec_inputs()

    def _L0_gnn_setup():
        import jax, jax.numpy as jnp
        import numpy as np
        N_NODES = 6250
        N_EDGES = 100000
        DIM = 96
        key = jax.random.key(seed)
        k = jax.random.split(key, 6)
        x = jax.random.normal(k[0], (N_NODES, DIM), dtype=jnp.float32)
        edge_index = jax.random.randint(k[1], (2, N_EDGES), 0, N_NODES, dtype=jnp.int64)
        edge_attr = jax.random.normal(k[2], (N_EDGES, DIM), dtype=jnp.float32)
        scale = 1.0 / np.sqrt(DIM)
        W1 = jax.random.normal(k[3], (DIM, DIM), dtype=jnp.float32) * scale
        b1 = jnp.zeros((DIM,), dtype=jnp.float32)
        W2 = jax.random.normal(k[4], (DIM, DIM), dtype=jnp.float32) * scale
        b2 = jnp.zeros((DIM,), dtype=jnp.float32)
        return {'x': x, 'edge_index': edge_index, 'edge_attr': edge_attr, 'W1': W1, 'b1': b1, 'W2': W2, 'b2': b2}
    _L0_gnn_all = _L0_gnn_setup()
    _L0_gnn_in = {k: v for k, v in _L0_gnn_all.items() if k in ('W1', 'b1', 'W2', 'b2')}
    del _L0_gnn_all
    return {'x': x, 'src': src, 'dst': dst, 'edge_attr_96': edge_attr_96, 'L0_gnn_W1': _L0_gnn_in['W1'], 'L0_gnn_b1': _L0_gnn_in['b1'], 'L0_gnn_W2': _L0_gnn_in['W2'], 'L0_gnn_b2': _L0_gnn_in['b2']}

def reference(x, src, dst, edge_attr_96, L0_gnn_W1, L0_gnn_b1, L0_gnn_W2, L0_gnn_b2):
    import jax
    import jax.numpy as jnp

    def _L0_gnn_ref(x, edge_index, edge_attr, W1, b1, W2, b2):
        import jax, jax.numpy as jnp
        import numpy as np
        N_NODES = 6250
        N_EDGES = 100000
        DIM = 96
        src = edge_index[0]
        dst = edge_index[1]
        msg = jax.nn.relu(x[src] + edge_attr)
        aggr = jax.ops.segment_sum(msg, dst, num_segments=x.shape[0])
        h = x + aggr
        h = jax.nn.relu(h @ W1 + b1) @ W2 + b2
        return x + jax.nn.relu(h)
    edge_index = jnp.stack([src, dst])
    h = jnp.maximum(_layernorm(x, axis=-1), 0.0)
    x = x + _L0_gnn_ref(h, edge_index, edge_attr_96, L0_gnn_W1, L0_gnn_b1, L0_gnn_W2, L0_gnn_b2)
    return x

_drawn_inputs = setup_inputs


def setup_inputs(seed=0):
    import zlib

    import numpy as np

    out = dict(_drawn_inputs(seed))
    spreads = {'L0_gnn_b1': (0.0, 0.8), 'L0_gnn_b2': (0.0, 0.793)}
    factors = {}
    for name, (base, spread) in spreads.items():
        noise = np.random.default_rng([zlib.crc32(name.encode()), seed]).standard_normal(out[name].shape)
        drawn = base * np.exp(spread * noise) if base else spread * noise
        out[name] = jnp.asarray(drawn.astype(out[name].dtype))
    for name, factor in factors.items():
        out[name] = (out[name] * factor).astype(out[name].dtype)
    return out
```

```python
from contextlib import ExitStack

import concourse.bass as bass
from concourse import mybir

F32 = mybir.dt.float32
I32 = mybir.dt.int32
ALU = mybir.AluOpType
ACT = mybir.ActivationFunctionType
AX = mybir.AxisListType


def gnn_kernel(nc, x, src, dst, edge_attr, W1, b1, W2, b2, out):
    N, D = x.shape
    E = src.shape[0]
    P = 128
    EPS = 1e-5

    EG = 10
    GE = EG * P
    NG = E // GE
    TE = E - NG * GE
    assert 0 < TE <= P and NG <= P and TE <= EG
    WIN = 128
    NS = 3
    FIRST = 0
    ROUNDS = (NG - 2) // NS
    PEELED = NG - ROUNDS * NS
    assert PEELED == 2

    NC = N // P
    NM = NC * P
    NT = N - NM
    NB = -(-N // WIN)
    QC = 4
    QN = NC // QC

    e_main = edge_attr[0:NG * GE, :].rearrange("(r j) d -> r (j d)", j=EG)
    x_main = x[0:NM, :].rearrange("(p c) d -> p (c d)", c=NC)
    out_main = out[0:NM, :].rearrange("(p c) d -> p (c d)", c=NC)
    src_main = src[0:NG * GE].rearrange("(r j) -> r j", j=EG)
    dst_main = dst[0:NG * GE].rearrange("(g e) -> g e", e=GE)

    with ExitStack() as ctx:
        def sb(name, shape, dt=F32):
            return ctx.enter_context(nc.sbuf_tensor(name, shape, dt))

        def ps(name, shape):
            return ctx.enter_context(nc.psum_tensor(name, shape, F32))

        def sem(name):
            return ctx.enter_context(nc.semaphore(name))

        def sems(name):
            return [sem(f"{name}{s}") for s in range(NS)]

        h_rows = nc.dram_tensor("h_rows", (N, D), F32, kind="Internal").ap()
        h_rows_main = h_rows[0:NM, :].rearrange("(p c) d -> p (c d)", c=NC)

        xm = sb("xm", [P, NC * D])
        xt = sb("xt", [P, D])
        hm = sb("hm", [P, NC * D])
        ht = sb("ht", [P, D])
        stats = sb("stats", [P, NC + 1, 6])
        mean = sb("mean", [P, NC + 1])
        var = sb("var", [P, NC + 1])
        dif = sb("dif", [P, NC + 1])
        rstd = sb("rstd", [P, NC + 1])
        shift = sb("shift", [P, NC + 1])
        eps = sb("eps", [P, 1])
        sums = sb("sums", [D, N + WIN])
        w1 = sb("w1", [D, D])
        w2b = sb("w2b", [D + 1, D])
        b1c = sb("b1c", [D, 1])
        act1 = [sb(f"act1_{k}", [D + 1, QC * P]) for k in range(2)]
        out_t = sb("out_t", [P, D])
        ident = sb("ident", [P, P])
        dst_row = sb("dst_row", [NG, GE], I32)
        dstf = sb("dstf", [NG, GE])
        rel_row = sb("rel_row", [NG, GE])
        far_row = sb("far_row", [NG, GE])
        base = sb("base", [NG, 1])
        top = sb("top", [NG, 1])
        span = sb("span", [NG, 1])
        relT = sb("relT", [P, NG, EG])
        tail_src = sb("tail_src", [TE, 1], I32)
        tail_dst = sb("tail_dst", [1, TE], I32)
        tail_dstf = sb("tail_dstf", [1, TE])
        tail_rel = sb("tail_rel", [1, TE])
        tail_far = sb("tail_far", [1, TE])
        tail_relT = sb("tail_relT", [TE, 1])
        tail_base = sb("tail_base", [1, 1])
        tail_top = sb("tail_top", [1, 1])
        spans = sb("spans", [1, NG + 1])
        widest = sb("widest", [1, 1])
        outside = sb("outside", [1, 1], I32)
        bases = sb("bases", [1, NG + 1], I32)
        node_id = sb("node_id", [P, WIN])
        block_id = sb("block_id", [P, WIN])
        idx = [sb(f"idx{s}", [P, EG], I32) for s in range(NS)]
        hsrc = [sb(f"hsrc{s}", [P, EG * D]) for s in range(NS)]
        msg = [sb(f"msg{s}", [P, EG * D]) for s in range(NS)]
        e_stats = [sb(f"e_stats{s}", [P, EG, 6]) for s in range(NS)]
        e_mean = [sb(f"e_mean{s}", [P, EG]) for s in range(NS)]
        e_var = [sb(f"e_var{s}", [P, EG]) for s in range(NS)]
        e_dif = [sb(f"e_dif{s}", [P, EG]) for s in range(NS)]
        e_rstd = [sb(f"e_rstd{s}", [P, EG]) for s in range(NS)]
        e_shift = [sb(f"e_shift{s}", [P, EG]) for s in range(NS)]
        pick = [sb(f"pick{s}", [P, EG, WIN]) for s in range(NS)]

        win_ps = [ps(f"win_ps{s}", [P, 512]) for s in range(NS)]
        tr_ps = [ps(f"tr_ps{k}", [P, 512]) for k in range(2)]
        y_ps = [ps(f"y_ps{k}", [P, 512]) for k in range(2)]

        edges_in = sem("edges_in")
        nodes_in = sem("nodes_in")
        weights_in = sem("weights_in")
        consts = sem("consts")
        zeroed = sem("zeroed")
        dve_prep = sem("dve_prep")
        xt_zeroed = sem("xt_zeroed")
        stats_done = sem("stats_done")
        var_done = sem("var_done")
        std_done = sem("std_done")
        scale_done = sem("scale_done")
        h_done = sem("h_done")
        h_stored = sem("h_stored")
        xh_done = sem("xh_done")
        rows_ready = sem("rows_ready")
        list_tr = sem("list_tr")
        list_copied = sem("list_copied")
        bases_tr = sem("bases_tr")
        bases_ready = sem("bases_ready")
        h_tr = sem("h_tr")
        h_copied = sem("h_copied")
        idx_in = sems("idx_in")
        e_stats_done = sems("e_stats_done")
        e_var_done = sems("e_var_done")
        e_std_done = sems("e_std_done")
        e_scale_done = sems("e_scale_done")
        e_h_done = sems("e_h_done")
        gathered = sems("gathered")
        attr_in = sems("attr_in")
        summed = sems("summed")
        relu_done = sems("relu_done")
        picked = sems("picked")
        multiplied = sems("multiplied")
        added = sems("added")
        far_rows = sem("far_rows")
        far_tr = sem("far_tr")
        far_copied = sem("far_copied")
        f_idx_in = sem("f_idx_in")
        f_gathered = sem("f_gathered")
        f_attr_in = sem("f_attr_in")
        f_summed = sem("f_summed")
        f_relu = sem("f_relu")
        f_block = sem("f_block")
        f_picked = sem("f_picked")
        f_multiplied = sem("f_multiplied")
        f_added = sem("f_added")
        sums_done = sem("sums_done")
        y1_ready = sem("y1_ready")
        act1_ready = sem("act1_ready")
        y2_ready = sem("y2_ready")
        out_ready = sem("out_ready")
        out_stored = sem("out_stored")

        LT = 5
        LB = EG // LT
        hcopy_steps = QN + 1

        block = ctx.enter_context(nc.Block())

        @block.sync
        def _(sp):
            def load_idx(g, s, rnd):
                sp.wait_ge(summed[s], rnd + 1)
                sp.dma_start(idx[s][:, :], src_main[bass.ds(g * P, P), :]).then_inc(idx_in[s], 16)

            def load_attr(g, s, rnd):
                if rnd is not FIRST:
                    sp.wait_ge(multiplied[s], rnd)
                sp.dma_start(msg[s][:, :], e_main[bass.ds(g * P, P), :]).then_inc(attr_in[s], 16)

            load_idx(0, 0, FIRST)
            sp.dma_start(xm[:, :], x_main).then_inc(nodes_in, 16)
            sp.wait_ge(xt_zeroed, 1)
            sp.dma_start(xt[0:NT, :], x[NM:N, :]).then_inc(nodes_in, 16)
            load_idx(1, 1, FIRST)
            load_idx(2, 2, FIRST)
            for s in range(NS):
                load_attr(s, s, FIRST)
            sp.dma_start(w1[:, :], W1[:, :]).then_inc(weights_in, 16)
            sp.dma_start(w2b[0:D, :], W2[:, :]).then_inc(weights_in, 16)
            sp.dma_start(w2b[D:D + 1, :], b2.rearrange("(o d) -> o d", o=1)).then_inc(weights_in, 16)
            sp.dma_start(b1c[:, :], b1.rearrange("(d o) -> d o", o=1)).then_inc(weights_in, 16)
            sp.wait_ge(h_done, NC + 1)
            sp.dma_start(h_rows_main, hm[:, :]).then_inc(h_stored, 16)
            sp.dma_start(h_rows[NM:N, :], ht[0:NT, :]).then_inc(h_stored, 16)
            with sp.Fori(1, ROUNDS) as i:
                for s in range(NS):
                    load_idx(i * NS + s, s, i)
                    load_attr(i * NS + s, s, i)
            for s in range(PEELED):
                load_idx(ROUNDS * NS + s, s, ROUNDS)
                load_attr(ROUNDS * NS + s, s, ROUNDS)
            sp.wait_ge(multiplied[PEELED], ROUNDS)
            sp.dma_start(msg[PEELED][0:TE, 0:D], edge_attr[NG * GE:E, :]).then_inc(attr_in[PEELED], 16)

            sp.wait_ge(bases_ready, 1)
            with sp.If(sp.value_load(outside[0:1, 0:1], min_val=0, max_val=1) == 1):
                sp.wait_ge(multiplied[0], ROUNDS + 1)
                with sp.Fori(1, NG + 1) as nth:
                    rows = bass.ds((nth - 1) * P, P)
                    sp.wait_ge(f_summed, nth)
                    sp.dma_start(idx[0][:, :], src_main[rows, :]).then_inc(f_idx_in, 16)
                    sp.wait_ge(f_added, (nth - 1) * NB + 1)
                    sp.dma_start(msg[0][:, :], e_main[rows, :]).then_inc(f_attr_in, 16)
                sp.wait_ge(f_added, NG * NB + 1)
                sp.dma_start(msg[0][0:TE, 0:D], edge_attr[NG * GE:E, :]).then_inc(f_attr_in, 16)

            SC = 2 * QC * D
            with sp.Fori(0, QN // 2) as q:
                sp.wait_ge(out_ready, q * 2 + 2)
                sp.dma_start(out_main[:, bass.ds(q * SC, SC)], xm[:, bass.ds(q * SC, SC)]).then_inc(out_stored, 16)
            sp.wait_ge(out_ready, QN + 1)
            sp.dma_start(out[NM:N, :], out_t[0:NT, :]).then_inc(out_stored, 16)
            sp.wait_ge(out_stored, 16 * (QN // 2 + 1))

        @block.gpsimd
        def _(pool):
            nc.gpsimd.iota(node_id[:, :], pattern=[[1, WIN]], base=0, channel_multiplier=0,
                           allow_small_or_imprecise_dtypes=True).then_inc(consts, 1)
            nc.gpsimd.memset(ident[:, :], 0.0).then_inc(zeroed, 1)
            pool.wait_ge(zeroed, 1)
            nc.gpsimd.affine_select(out=ident[:, :], in_=ident[:, :], compare_op=ALU.not_equal, fill=1.0,
                                    base=0, pattern=[[-1, P]], channel_multiplier=1).then_inc(consts, 1)
            def gather(idx_s, hsrc_s, done):
                for j in range(EG):
                    nc.gpsimd.indirect_dma_start(
                        out=hsrc_s[:, j * D:(j + 1) * D], out_offset=None, in_=h_rows,
                        in_offset=bass.IndirectOffsetOnAxis(ap=idx_s[:, j:j + 1], axis=0),
                    ).then_inc(done, 16)

            for s in range(NS):
                pool.wait_ge(idx_in[s], 16)
                for j in range(EG):
                    nc.gpsimd.indirect_dma_start(
                        out=hsrc[s][:, j * D:(j + 1) * D], out_offset=None, in_=x,
                        in_offset=bass.IndirectOffsetOnAxis(ap=idx[s][:, j:j + 1], axis=0),
                    ).then_inc(gathered[s], 16)
            with pool.Fori(2 * 16, (ROUNDS + 1) * 16, 16) as arrived:
                for s in range(NS):
                    pool.wait_ge(h_stored, 32)
                    pool.wait_ge(idx_in[s], arrived)
                    gather(idx[s], hsrc[s], gathered[s])
            for s in range(PEELED):
                pool.wait_ge(idx_in[s], (ROUNDS + 1) * 16)
                gather(idx[s], hsrc[s], gathered[s])
            pool.wait_ge(summed[PEELED], ROUNDS + 1)
            pool.wait_ge(edges_in, 48)
            nc.gpsimd.indirect_dma_start(
                out=hsrc[PEELED][0:TE, 0:D], out_offset=None, in_=h_rows,
                in_offset=bass.IndirectOffsetOnAxis(ap=tail_src[:, 0:1], axis=0),
            ).then_inc(gathered[PEELED], 16)

            pool.wait_ge(bases_ready, 1)
            with pool.If(pool.value_load(outside[0:1, 0:1], min_val=0, max_val=1) == 1):
                with pool.Fori(16, (NG + 1) * 16, 16) as arrived:
                    pool.wait_ge(h_stored, 32)
                    pool.wait_ge(f_idx_in, arrived)
                    gather(idx[0], hsrc[0], f_gathered)
                pool.wait_ge(f_summed, NG + 1)
                nc.gpsimd.indirect_dma_start(
                    out=hsrc[0][0:TE, 0:D], out_offset=None, in_=h_rows,
                    in_offset=bass.IndirectOffsetOnAxis(ap=tail_src[:, 0:1], axis=0),
                ).then_inc(f_gathered, 16)

        @block.scalar
        def _(act):
            act.dma_start(dst_row[:, :], dst_main).then_inc(edges_in, 16)
            act.dma_start(tail_src[:, :], src[NG * GE:E].rearrange("(e o) -> e o", o=1)).then_inc(edges_in, 16)
            act.dma_start(tail_dst[:, :], dst[NG * GE:E].rearrange("(o e) -> o e", o=1)).then_inc(edges_in, 16)

            act.wait_ge(var_done, 1)
            nc.scalar.activation(rstd[:, :], var[:, :], ACT.Sqrt, bias=eps[:, 0:1]).then_inc(std_done, 1)
            act.wait_ge(scale_done, 1)
            with act.Fori(0, NC // 8) as i:
                for k in range(8):
                    c = i * 8 + k
                    nc.scalar.activation(hm[:, bass.ds(c * D, D)], xm[:, bass.ds(c * D, D)], ACT.Relu,
                                         bias=shift[:, bass.ds(c, 1)], scale=rstd[:, bass.ds(c, 1)],
                                         ).then_inc(h_done, 1)
            nc.scalar.activation(ht[0:NT, :], xt[0:NT, :], ACT.Relu, bias=shift[0:NT, NC:NC + 1],
                                 scale=rstd[0:NT, NC:NC + 1]).then_inc(h_done, 1)

            def relu(s, rnd):
                act.wait_ge(summed[s], rnd + 2)
                nc.scalar.activation(msg[s][:, :], msg[s][:, :], ACT.Relu).then_inc(relu_done[s], 1)

            def normalise_rows(s):
                act.wait_ge(e_var_done[s], 1)
                nc.scalar.activation(e_rstd[s][:, :], e_var[s][:, :], ACT.Sqrt, bias=eps[:, 0:1]
                                     ).then_inc(e_std_done[s], 1)
                act.wait_ge(e_scale_done[s], 1)
                for j in range(EG):
                    row = hsrc[s][:, j * D:(j + 1) * D]
                    nc.scalar.activation(row, row, ACT.Relu, bias=e_shift[s][:, j:j + 1],
                                         scale=e_rstd[s][:, j:j + 1]).then_inc(e_h_done[s], 1)

            normalise_rows(0)
            smain = sums[:, 0:NM].rearrange("f (p c) -> f c p", c=NC)
            for q in range(QN):
                act.wait_ge(h_tr, q + 1)
                nc.scalar.copy(smain[:, q * QC:(q + 1) * QC, :],
                               tr_ps[q % 2][0:D, 0:QC * P].rearrange("f (c p) -> f c p", c=QC)).then_inc(h_copied, 1)
            act.wait_ge(h_tr, QN + 1)
            nc.scalar.copy(sums[:, NM:N], tr_ps[QN % 2][0:D, 0:NT]).then_inc(h_copied, 1)
            relu(0, FIRST)
            for s in range(1, NS):
                normalise_rows(s)
                relu(s, FIRST)

            with act.Fori(1, ROUNDS) as i:
                for s in range(NS):
                    relu(s, i)
            for s in range(PEELED):
                relu(s, ROUNDS)
            act.wait_ge(summed[PEELED], ROUNDS + 2)
            nc.scalar.activation(msg[PEELED][0:TE, 0:D], msg[PEELED][0:TE, 0:D], ACT.Relu
                                 ).then_inc(relu_done[PEELED], 1)

            act.wait_ge(bases_ready, 1)
            with act.If(act.value_load(outside[0:1, 0:1], min_val=0, max_val=1) == 1):
                with act.Fori(0, NG) as g:
                    act.wait_ge(f_summed, g + 2)
                    nc.scalar.activation(msg[0][:, :], msg[0][:, :], ACT.Relu).then_inc(f_relu, 1)
                act.wait_ge(f_summed, NG + 2)
                nc.scalar.activation(msg[0][0:TE, 0:D], msg[0][0:TE, 0:D], ACT.Relu).then_inc(f_relu, 1)

            act.wait_ge(weights_in, 64)
            with act.Fori(0, QN // 2) as q:
                for k in range(2):
                    act.wait_ge(y1_ready, q * 2 + k + 1)
                    nc.scalar.activation(act1[k][0:D, :], tr_ps[k][0:D, :], ACT.Relu, bias=b1c[:, 0:1]
                                         ).then_inc(act1_ready, 1)
            act.wait_ge(y1_ready, QN + 1)
            nc.scalar.activation(act1[0][0:D, 0:NT], tr_ps[0][0:D, 0:NT], ACT.Relu, bias=b1c[:, 0:1]
                                 ).then_inc(act1_ready, 1)

        @block.vector
        def _(dve):
            steps = [0]

            def then(ins):
                steps[0] += 1
                ins.then_inc(dve_prep, 1)
                dve.wait_ge(dve_prep, steps[0])

            nc.vector.memset(xt[:, :], 0.0).then_inc(xt_zeroed, 1)
            for s in range(NS):
                nc.vector.memset(hsrc[s][:, 0:1], 0.0).then_inc(summed[s], 1)
            nc.vector.memset(eps[:, :], EPS).then_inc(f_summed, 1)
            nc.vector.memset(act1[0][D:D + 1, :], 1.0)
            nc.vector.memset(act1[1][D:D + 1, :], 1.0)
            nc.vector.memset(sums[:, N:N + WIN], 0.0)

            dve.wait_ge(edges_in, 48)
            nc.vector.tensor_copy(tail_dstf[:, :], tail_dst[:, :])
            then(nc.vector.tensor_copy(dstf[:, :], dst_row[:, :]))
            nc.vector.tensor_reduce(base[:, :], dstf[:, :], AX.X, ALU.min)
            nc.vector.tensor_reduce(tail_base[:, :], tail_dstf[:, :], AX.X, ALU.min)
            nc.vector.tensor_reduce(tail_top[:, :], tail_dstf[:, :], AX.X, ALU.max)
            then(nc.vector.tensor_reduce(top[:, :], dstf[:, :], AX.X, ALU.max))
            nc.vector.tensor_scalar(rel_row[:, :], dstf[:, :], base[:, 0:1], None, ALU.subtract)
            nc.vector.tensor_copy(bases[0:1, NG:NG + 1], tail_base[:, :])
            nc.vector.tensor_tensor(spans[0:1, NG:NG + 1], tail_top[:, :], tail_base[:, :], ALU.subtract)
            nc.vector.tensor_scalar(tail_rel[:, :], tail_dstf[:, :], tail_base[:, 0:1], None, ALU.subtract)
            nc.vector.tensor_tensor(span[:, :], top[:, :], base[:, :], ALU.subtract).then_inc(rows_ready, 1)

            def row_variance(stats, mean, dif, var, done):
                mean_e, ssq_e, mean_o, ssq_o = (stats[:, :, k] for k in (1, 2, 4, 5))
                nc.vector.tensor_tensor(mean[:, :], mean_e, mean_o, ALU.add)
                nc.vector.tensor_tensor(dif[:, :], mean_e, mean_o, ALU.subtract)
                then(nc.vector.tensor_tensor(var[:, :], ssq_e, ssq_o, ALU.add))
                nc.vector.tensor_scalar(mean[:, :], mean[:, :], 0.5, None, ALU.mult)
                nc.vector.tensor_scalar(var[:, :], var[:, :], 1.0 / D, None, ALU.mult)
                then(nc.vector.scalar_tensor_tensor(dif[:, :], dif[:, :], 0.25, dif[:, :], ALU.mult, ALU.mult))
                nc.vector.tensor_tensor(var[:, :], var[:, :], dif[:, :], ALU.add).then_inc(done, 1)

            def row_scale(mean, rstd, shift, done):
                then(nc.vector.reciprocal(rstd[:, :], rstd[:, :]))
                nc.vector.scalar_tensor_tensor(shift[:, :], mean[:, :], -1.0, rstd[:, :], ALU.mult, ALU.mult
                                               ).then_inc(done, 1)

            dve.wait_ge(nodes_in, 32)
            with dve.Fori(0, NC // 8) as i:
                for k in range(8):
                    c = i * 8 + k
                    nc.vector.bn_stats(stats[:, bass.ds(c, 1), :].rearrange("p c s -> p (c s)"),
                                       xm[:, bass.ds(c * D, D)]).then_inc(stats_done, 1)
            nc.vector.bn_stats(stats[:, NC, :], xt[:, :]).then_inc(stats_done, 1)
            dve.wait_ge(stats_done, NC + 1)
            row_variance(stats, mean, dif, var, var_done)
            dve.wait_ge(std_done, 1)
            row_scale(mean, rstd, shift, scale_done)

            for k in range(LB):
                dve.wait_ge(list_tr, k + 1)
                nc.vector.tensor_copy(relT[:, :, k * LT:(k + 1) * LT],
                                      tr_ps[k % 2][:, 0:LT * NG].rearrange("p (j g) -> p g j", j=LT)
                                      ).then_inc(list_copied, 1)
            dve.wait_ge(bases_tr, 1)
            nc.vector.tensor_copy(bases[0:1, 0:NG], y_ps[0][0:1, 0:NG])
            nc.vector.tensor_copy(spans[0:1, 0:NG], y_ps[0][0:1, P:P + NG])
            then(nc.vector.tensor_copy(tail_relT[:, :], y_ps[0][0:TE, 2 * P:2 * P + 1]))
            then(nc.vector.tensor_reduce(widest[:, :], spans[:, :], AX.X, ALU.max))
            nc.vector.tensor_scalar(outside[:, :], widest[:, :], float(WIN), None, ALU.is_ge).then_inc(bases_ready, 1)

            def row_moments(s):
                dve.wait_ge(gathered[s], 16 * EG)
                for j in range(EG):
                    nc.vector.bn_stats(e_stats[s][:, j, :], hsrc[s][:, j * D:(j + 1) * D]).then_inc(e_stats_done[s], 1)
                dve.wait_ge(e_stats_done[s], EG)
                row_variance(e_stats[s], e_mean[s], e_dif[s], e_var[s], e_var_done[s])
                dve.wait_ge(e_std_done[s], 1)
                row_scale(e_mean[s], e_rstd[s], e_shift[s], e_scale_done[s])

            dve.wait_ge(consts, 2)
            dve.wait_ge(list_copied, LB)
            dve.wait_ge(bases_ready, 1)

            def group(g, s, rnd):
                if rnd is not FIRST:
                    dve.wait_ge(multiplied[s], rnd)
                nc.vector.tensor_tensor(
                    pick[s][:, :, :], node_id[:, :].unsqueeze(1).broadcast_to([P, EG, WIN]),
                    relT[:, bass.ds(g, 1), :].rearrange("p g j -> p (g j)").unsqueeze(2).broadcast_to([P, EG, WIN]),
                    ALU.is_equal).then_inc(picked[s], 1)
                dve.wait_ge(attr_in[s], 16 * (rnd + 1))
                if rnd is FIRST:
                    row_moments(s)
                    dve.wait_ge(e_h_done[s], EG)
                else:
                    dve.wait_ge(gathered[s], 16 * EG * (rnd + 1))
                nc.vector.tensor_tensor(msg[s][:, :], msg[s][:, :], hsrc[s][:, :], ALU.add).then_inc(summed[s], 1)
                first = dve.value_load(bases[0:1, bass.ds(g, 1)], min_val=0, max_val=N - 1)
                dve.wait_ge(multiplied[s], rnd + 1)
                if s > 0:
                    dve.wait_ge(added[s - 1], rnd + 1)
                elif rnd is not FIRST:
                    dve.wait_ge(added[NS - 1], rnd)
                else:
                    dve.wait_ge(h_copied, hcopy_steps)
                nc.vector.tensor_tensor(sums[:, bass.ds(first, WIN)], sums[:, bass.ds(first, WIN)],
                                        win_ps[s][0:D, 0:WIN], ALU.add).then_inc(added[s], 1)

            for s in range(NS):
                group(s, s, FIRST)
            dve.wait_ge(h_done, NC + 1)
            nc.vector.tensor_tensor(xm[:, :], xm[:, :], hm[:, :], ALU.add)
            nc.vector.tensor_tensor(xt[0:NT, :], xt[0:NT, :], ht[0:NT, :], ALU.add).then_inc(xh_done, 1)
            with dve.Fori(1, ROUNDS) as i:
                for s in range(NS):
                    group(i * NS + s, s, i)
            for s in range(PEELED):
                group(ROUNDS * NS + s, s, ROUNDS)
            s = PEELED
            dve.wait_ge(multiplied[s], ROUNDS)
            nc.vector.tensor_scalar(pick[s][0:TE, 0, :], node_id[0:TE, :], tail_relT[:, 0:1], None,
                                    ALU.is_equal).then_inc(picked[s], 1)
            dve.wait_ge(attr_in[s], 16 * (ROUNDS + 1))
            dve.wait_ge(gathered[s], 16 * EG * ROUNDS + 16)
            nc.vector.tensor_tensor(msg[s][0:TE, 0:D], msg[s][0:TE, 0:D], hsrc[s][0:TE, 0:D], ALU.add
                                    ).then_inc(summed[s], 1)
            first = dve.value_load(bases[0:1, NG:NG + 1], min_val=0, max_val=N - 1)
            dve.wait_ge(multiplied[s], ROUNDS + 1)
            dve.wait_ge(added[s - 1], ROUNDS + 1)
            nc.vector.tensor_tensor(sums[:, bass.ds(first, WIN)], sums[:, bass.ds(first, WIN)],
                                    win_ps[s][0:D, 0:WIN], ALU.add).then_inc(added[s], 1)
            dve.wait_ge(added[s], ROUNDS + 1)

            with dve.If(dve.value_load(outside[0:1, 0:1], min_val=0, max_val=1) == 1):
                nc.vector.tensor_scalar(far_row[:, :], rel_row[:, :], float(WIN), None, ALU.is_ge)
                nc.vector.tensor_scalar(tail_far[:, :], tail_rel[:, :], float(WIN), None, ALU.is_ge)
                nc.vector.tensor_scalar(dstf[:, :], dstf[:, :], 1.0, None, ALU.add)
                then(nc.vector.tensor_scalar(tail_dstf[:, :], tail_dstf[:, :], 1.0, None, ALU.add))
                nc.vector.tensor_tensor(far_row[:, :], far_row[:, :], dstf[:, :], ALU.mult)
                then(nc.vector.tensor_tensor(tail_far[:, :], tail_far[:, :], tail_dstf[:, :], ALU.mult))
                nc.vector.tensor_scalar(far_row[:, :], far_row[:, :], -1.0, None, ALU.add)
                nc.vector.tensor_scalar(tail_far[:, :], tail_far[:, :], -1.0, None, ALU.add
                                        ).then_inc(far_rows, 1)
                nc.vector.tensor_copy(block_id[:, :], node_id[:, :]).then_inc(f_block, 1)
                nc.vector.memset(eps[:, :], EPS).then_inc(f_added, 1)
                for k in range(LB):
                    dve.wait_ge(far_tr, k + 1)
                    nc.vector.tensor_copy(relT[:, :, k * LT:(k + 1) * LT],
                                          tr_ps[k % 2][:, 0:LT * NG].rearrange("p (j g) -> p g j", j=LT)
                                          ).then_inc(far_copied, 1)
                dve.wait_ge(far_tr, LB + 1)
                nc.vector.tensor_copy(tail_relT[:, :], y_ps[0][0:TE, 0:1]).then_inc(far_copied, 1)
                dve.wait_ge(far_copied, LB + 1)

                def restart(nth):
                    dve.wait_ge(f_block, (nth - 1) * (NB + 1) + 1)
                    nc.vector.tensor_copy(block_id[:, :], node_id[:, :]).then_inc(f_block, 1)

                def add_block(nth, w, whole):
                    dve.wait_ge(f_block, (nth - 1) * (NB + 1) + w + 2)
                    if whole:
                        nc.vector.tensor_tensor(
                            pick[0][:, :, :], block_id[:, :].unsqueeze(1).broadcast_to([P, EG, WIN]),
                            relT[:, bass.ds(nth - 1, 1), :].rearrange("p g j -> p (g j)").unsqueeze(2)
                            .broadcast_to([P, EG, WIN]), ALU.is_equal).then_inc(f_picked, 1)
                    else:
                        nc.vector.tensor_scalar(pick[0][0:TE, 0, :], block_id[0:TE, :], tail_relT[:, 0:1], None,
                                                ALU.is_equal).then_inc(f_picked, 1)
                    done = (nth - 1) * NB + w + 1
                    dve.wait_ge(f_picked, done)
                    nc.vector.tensor_scalar(block_id[:, :], block_id[:, :], float(WIN), None, ALU.add
                                            ).then_inc(f_block, 1)
                    dve.wait_ge(f_multiplied, done)
                    dve.wait_ge(f_added, done)
                    nc.vector.tensor_tensor(sums[:, bass.ds(w * WIN, WIN)], sums[:, bass.ds(w * WIN, WIN)],
                                            win_ps[0][0:D, 0:WIN], ALU.add).then_inc(f_added, 1)

                with dve.Fori(1, NG + 1) as nth:
                    dve.wait_ge(f_attr_in, 16 * nth)
                    dve.wait_ge(f_gathered, 16 * EG * nth)
                    nc.vector.tensor_tensor(msg[0][:, :], msg[0][:, :], hsrc[0][:, :], ALU.add).then_inc(f_summed, 1)
                    restart(nth)
                    with dve.Fori(0, NB) as w:
                        add_block(nth, w, True)
                dve.wait_ge(f_attr_in, 16 * (NG + 1))
                dve.wait_ge(f_gathered, 16 * EG * NG + 16)
                nc.vector.tensor_tensor(msg[0][0:TE, 0:D], msg[0][0:TE, 0:D], hsrc[0][0:TE, 0:D], ALU.add
                                        ).then_inc(f_summed, 1)
                restart(NG + 1)
                with dve.Fori(0, NB) as w:
                    add_block(NG + 1, w, False)
                dve.wait_ge(f_added, (NG + 1) * NB + 1)
            nc.vector.memset(e_dif[0][:, :], 0.0).then_inc(sums_done, 1)

            dve.wait_ge(xh_done, 1)
            with dve.Fori(0, QN // 2) as q:
                for k in range(2):
                    cols = bass.ds((q * 2 + k) * QC * D, QC * D)
                    dve.wait_ge(y2_ready, q * 2 + k + 1)
                    nc.vector.scalar_tensor_tensor(xm[:, cols], y_ps[k][:, 0:QC * D], 0.0, xm[:, cols],
                                                   ALU.max, ALU.add).then_inc(out_ready, 1)
            dve.wait_ge(y2_ready, QN + 1)
            nc.vector.scalar_tensor_tensor(out_t[0:NT, :], y_ps[0][0:NT, 0:D], 0.0, xt[0:NT, :],
                                           ALU.max, ALU.add).then_inc(out_ready, 1)

        @block.tensor
        def _(pe):
            pe.wait_ge(consts, 2)
            pe.wait_ge(rows_ready, 1)
            rows = rel_row[:, :].rearrange("g (p j) -> g j p", j=EG)
            for k in range(LB):
                for t in range(LT):
                    last = nc.tensor.transpose(tr_ps[k % 2][:, t * NG:(t + 1) * NG], rows[:, k * LT + t, :],
                                               ident[0:NG, 0:NG])
                last.then_inc(list_tr, 1)
            nc.tensor.transpose(y_ps[0][0:1, 0:NG], base[:, 0:1], ident[0:NG, 0:NG])
            nc.tensor.transpose(y_ps[0][0:1, P:P + NG], span[:, 0:1], ident[0:NG, 0:NG])
            nc.tensor.transpose(y_ps[0][0:TE, 2 * P:2 * P + 1], tail_rel[:, :], ident[0:1, 0:1]
                                ).then_inc(bases_tr, 1)

            pe.wait_ge(list_copied, LB)
            pe.wait_ge(h_done, NC + 1)
            for q in range(QN):
                if q >= 2:
                    pe.wait_ge(h_copied, q - 1)
                for t in range(QC):
                    c = q * QC + t
                    last = nc.tensor.transpose(tr_ps[q % 2][0:D, t * P:(t + 1) * P], hm[:, c * D:(c + 1) * D],
                                               ident[:, :])
                last.then_inc(h_tr, 1)
            pe.wait_ge(h_copied, QN - 1)
            nc.tensor.transpose(tr_ps[QN % 2][0:D, 0:NT], ht[0:NT, :], ident[0:NT, 0:NT]).then_inc(h_tr, 1)

            def window(s, rnd):
                pe.wait_ge(picked[s], rnd + 1)
                if rnd is not FIRST:
                    pe.wait_ge(added[s], rnd)
                pe.wait_ge(relu_done[s], rnd + 1)
                for j in range(EG):
                    last = nc.tensor.matmul(win_ps[s][0:D, 0:WIN], msg[s][:, j * D:(j + 1) * D], pick[s][:, j, :],
                                            start=(j == 0), stop=(j == EG - 1))
                last.then_inc(multiplied[s], 1)

            for s in range(NS):
                window(s, FIRST)
            with pe.Fori(1, ROUNDS) as i:
                for s in range(NS):
                    window(s, i)
            for s in range(PEELED):
                window(s, ROUNDS)
            s = PEELED
            pe.wait_ge(picked[s], ROUNDS + 1)
            pe.wait_ge(added[s], ROUNDS)
            pe.wait_ge(relu_done[s], ROUNDS + 1)
            nc.tensor.matmul(win_ps[s][0:D, 0:WIN], msg[s][0:TE, 0:D], pick[s][0:TE, 0, :], start=True, stop=True
                             ).then_inc(multiplied[s], 1)

            pe.wait_ge(bases_ready, 1)
            with pe.If(pe.value_load(outside[0:1, 0:1], min_val=0, max_val=1) == 1):
                pe.wait_ge(far_rows, 1)
                rows = far_row[:, :].rearrange("g (p j) -> g j p", j=EG)
                for k in range(LB):
                    for t in range(LT):
                        last = nc.tensor.transpose(tr_ps[k % 2][:, t * NG:(t + 1) * NG], rows[:, k * LT + t, :],
                                                   ident[0:NG, 0:NG])
                    last.then_inc(far_tr, 1)
                nc.tensor.transpose(y_ps[0][0:TE, 0:1], tail_far[:, :], ident[0:1, 0:1]).then_inc(far_tr, 1)
                pe.wait_ge(far_copied, LB + 1)
                with pe.Fori(1, NG + 1) as nth:
                    pe.wait_ge(far_rows, 1)
                    pe.wait_ge(f_relu, nth)
                    with pe.Fori(0, NB) as w:
                        pe.wait_ge(f_picked, (nth - 1) * NB + w + 1)
                        pe.wait_ge(f_added, (nth - 1) * NB + w + 1)
                        for j in range(EG):
                            last = nc.tensor.matmul(win_ps[0][0:D, 0:WIN], msg[0][:, j * D:(j + 1) * D],
                                                    pick[0][:, j, :], start=(j == 0), stop=(j == EG - 1))
                        last.then_inc(f_multiplied, 1)
                pe.wait_ge(f_relu, NG + 1)
                with pe.Fori(0, NB) as w:
                    pe.wait_ge(f_picked, NG * NB + w + 1)
                    pe.wait_ge(f_added, NG * NB + w + 1)
                    nc.tensor.matmul(win_ps[0][0:D, 0:WIN], msg[0][0:TE, 0:D], pick[0][0:TE, 0, :],
                                     start=True, stop=True).then_inc(f_multiplied, 1)

            pe.wait_ge(weights_in, 64)
            pe.wait_ge(sums_done, 1)
            smain = sums[:, 0:NM].rearrange("f (p c) -> f c p", c=NC)

            def second_layer(k, cols):
                for t in range(cols):
                    last = nc.tensor.matmul(y_ps[k][:, t * D:(t + 1) * D], act1[k][:, t * P:(t + 1) * P],
                                            w2b[:, :], start=True, stop=True)
                last.then_inc(y2_ready, 1)

            def layers(q):
                for k in range(2):
                    if q is not FIRST:
                        pe.wait_ge(act1_ready, q * 2)
                    nc.tensor.matmul(tr_ps[k][0:D, :], w1[:, :], smain[:, bass.ds((q * 2 + k) * QC, QC), :],
                                     start=True, stop=True).then_inc(y1_ready, 1)
                for k in range(2):
                    pe.wait_ge(act1_ready, q * 2 + k + 1)
                    if q is not FIRST:
                        pe.wait_ge(out_ready, q * 2)
                    second_layer(k, QC)

            layers(FIRST)
            with pe.Fori(1, QN // 2) as q:
                layers(q)
            pe.wait_ge(act1_ready, QN)
            nc.tensor.matmul(tr_ps[0][0:D, 0:NT], w1[:, :], sums[:, NM:N], start=True, stop=True).then_inc(y1_ready, 1)
            pe.wait_ge(act1_ready, QN + 1)
            pe.wait_ge(out_ready, QN)
            nc.tensor.matmul(y_ps[0][0:NT, 0:D], act1[0][:, 0:NT], w2b[:, :], start=True, stop=True).then_inc(y2_ready, 1)


_INS = ["x", "src", "dst", "edge_attr_96", "L0_gnn_W1", "L0_gnn_b1", "L0_gnn_W2", "L0_gnn_b2"]


def kernel(**inputs):
    import numpy as _np
    import concourse.bacc as _bacc
    from concourse.bass_utils import run_bass_kernel_spmd as _run

    nc = _bacc.Bacc("TRN2", target_bir_lowering=False, num_devices=1)
    arrays, args = {}, []
    for name in _INS:
        a = _np.ascontiguousarray(inputs[name])
        arrays[name] = a
        args.append(nc.dram_tensor(name, a.shape, mybir.dt.from_np(a.dtype), kind="ExternalInput").ap())
    args.append(nc.dram_tensor("out", arrays["x"].shape, F32, kind="ExternalOutput").ap())
    gnn_kernel(nc, *args)
    r = _run(nc, [arrays], core_ids=[0])
    return r.results[0]["out"]
```

```python
from contextlib import ExitStack

import concourse.bass as bass
from concourse import mybir

F32 = mybir.dt.float32
I32 = mybir.dt.int32
ALU = mybir.AluOpType
ACT = mybir.ActivationFunctionType
AX = mybir.AxisListType


def gnn_kernel(nc, x, src, dst, edge_attr, W1, b1, W2, b2, out):
    N, D = x.shape
    E = src.shape[0]
    P = 128
    EPS = 1e-5

    EG = 10
    GE = EG * P
    NG = E // GE
    TE = E - NG * GE
    assert 0 < TE <= P and NG <= P and TE <= EG
    WIN = 128
    NS = 4
    FIRST = 0
    ROUNDS = (NG - 1) // NS
    PEELED = NG - ROUNDS * NS
    assert 1 < PEELED < NS

    BC = 3
    BN = BC * P
    NJ = N // BN
    NC = NJ * BC
    NM = NJ * BN
    NT = N - NM
    HC = NC // 2
    NB = -(-N // WIN)
    LAG = 5
    EARLY = ROUNDS - LAG
    AJ = 2
    assert 0 < NT <= P and NJ % 2 == 0 and EARLY < NJ

    e_main = edge_attr[0:NG * GE, :].rearrange("(r j) d -> r (j d)", j=EG)
    x_main = x[0:NM, :].rearrange("(j p t) d -> p j (t d)", p=P, t=BC)
    out_main = out[0:NM, :].rearrange("(j p t) d -> p j (t d)", p=P, t=BC)
    src_main = src[0:NG * GE].rearrange("(r j) -> r j", j=EG)
    dst_main = dst[0:NG * GE].rearrange("(g e) -> g e", e=GE)

    with ExitStack() as ctx:
        def sb(name, shape, dt=F32):
            return ctx.enter_context(nc.sbuf_tensor(name, shape, dt))

        def ps(name, shape):
            return ctx.enter_context(nc.psum_tensor(name, shape, F32))

        def sem(name):
            return ctx.enter_context(nc.semaphore(name))

        def sems(name):
            return [sem(f"{name}{s}") for s in range(NS)]

        h_rows = nc.dram_tensor("h_rows", (N, D), F32, kind="Internal").ap()
        h_rows_main = h_rows[0:NM, :].rearrange("(j p t) d -> p j (t d)", p=P, t=BC)

        xm = sb("xm", [P, NJ, BC * D])
        xt = sb("xt", [P, D])
        hm = sb("hm", [P, NJ, BC * D])
        ht = sb("ht", [P, D])
        stats = sb("stats", [P, NC + 1, 6])
        mean = sb("mean", [P, NC + 1])
        var = sb("var", [P, NC + 1])
        dif = sb("dif", [P, NC + 1])
        rstd = sb("rstd", [P, NC + 1])
        shift = sb("shift", [P, NC + 1])
        eps = sb("eps", [P, 1])
        sums = sb("sums", [D, N + WIN])
        w1 = sb("w1", [D, D])
        w2b = sb("w2b", [D + 1, D])
        b1c = sb("b1c", [D, 1])
        act1 = [sb(f"act1_{k}", [D + 1, BN]) for k in range(2)]
        out_t = sb("out_t", [P, D])
        ident = sb("ident", [P, P])
        dst_row = sb("dst_row", [NG, GE], I32)
        dstf = sb("dstf", [NG, GE])
        rel_row = sb("rel_row", [NG, GE])
        far_row = sb("far_row", [NG, GE])
        base = sb("base", [NG, 1])
        top = sb("top", [NG, 1])
        span = sb("span", [NG, 1])
        relT = sb("relT", [P, NG, EG])
        tail_src = sb("tail_src", [TE, 1], I32)
        tail_dst = sb("tail_dst", [1, TE], I32)
        tail_dstf = sb("tail_dstf", [1, TE])
        tail_rel = sb("tail_rel", [1, TE])
        tail_far = sb("tail_far", [1, TE])
        tail_relT = sb("tail_relT", [TE, 1])
        tail_base = sb("tail_base", [1, 1])
        tail_top = sb("tail_top", [1, 1])
        spans = sb("spans", [1, NG + 1])
        widest = sb("widest", [1, 1])
        outside = sb("outside", [1, 1], I32)
        least = sb("least", [1, (ROUNDS + 2) * NS])
        passed = sb("passed", [1, NG])
        early = sb("early", [1, 1])
        redo = sb("redo", [1, 1], I32)
        bases = sb("bases", [1, NG + 1], I32)
        node_id = sb("node_id", [P, WIN])
        block_id = sb("block_id", [P, WIN])
        idx = [sb(f"idx{s}", [P, EG], I32) for s in range(NS)]
        hsrc = [sb(f"hsrc{s}", [P, EG * D]) for s in range(NS)]
        msg = [sb(f"msg{s}", [P, EG * D]) for s in range(NS)]
        t_hsrc = sb("t_hsrc", [TE, D])
        t_msg = sb("t_msg", [TE, D])
        t_pick = sb("t_pick", [TE, WIN])
        e_stats = [sb(f"e_stats{s}", [P, EG, 6]) for s in range(NS)]
        e_mean = [sb(f"e_mean{s}", [P, EG]) for s in range(NS)]
        e_var = [sb(f"e_var{s}", [P, EG]) for s in range(NS)]
        e_dif = [sb(f"e_dif{s}", [P, EG]) for s in range(NS)]
        e_rstd = [sb(f"e_rstd{s}", [P, EG]) for s in range(NS)]
        e_shift = [sb(f"e_shift{s}", [P, EG]) for s in range(NS)]
        pick = [sb(f"pick{s}", [P, EG, WIN]) for s in range(NS)]

        win_ps = [ps(f"win_ps{s}", [P, 512]) for s in range(NS)]
        tr_ps = [ps(f"tr_ps{k}", [P, 512]) for k in range(2)]
        y_ps = [ps(f"y_ps{k}", [P, 512]) for k in range(2)]

        edges_in = sem("edges_in")
        half_in = [sem(f"half_in{k}") for k in range(2)]
        tail_in = sem("tail_in")
        weights_in = sem("weights_in")
        consts = sem("consts")
        zeroed = sem("zeroed")
        dve_prep = sem("dve_prep")
        xt_zeroed = sem("xt_zeroed")
        stats_done = sem("stats_done")
        var_done = sem("var_done")
        std_done = sem("std_done")
        scale_ready = sem("scale_ready")
        scaled = sem("scaled")
        h_done = sem("h_done")
        h_stored = sem("h_stored")
        xh_done = sem("xh_done")
        rows_ready = sem("rows_ready")
        list_tr = sem("list_tr")
        list_copied = sem("list_copied")
        bases_tr = sem("bases_tr")
        bases_ready = sem("bases_ready")
        h_tr = sem("h_tr")
        h_copied = sem("h_copied")
        idx_in = sems("idx_in")
        e_stats_done = sems("e_stats_done")
        e_var_done = sems("e_var_done")
        e_std_done = sems("e_std_done")
        e_scale_done = sems("e_scale_done")
        e_scaled = sems("e_scaled")
        gathered = sems("gathered")
        attr_in = sems("attr_in")
        summed = sems("summed")
        relu_done = sems("relu_done")
        picked = sems("picked")
        multiplied = sems("multiplied")
        added = sems("added")
        t_attr_in = sem("t_attr_in")
        t_gathered = sem("t_gathered")
        t_summed = sem("t_summed")
        t_relu = sem("t_relu")
        t_picked = sem("t_picked")
        t_multiplied = sem("t_multiplied")
        t_added = sem("t_added")
        far_rows = sem("far_rows")
        far_tr = sem("far_tr")
        far_copied = sem("far_copied")
        f_idx_in = sem("f_idx_in")
        f_gathered = sem("f_gathered")
        f_attr_in = sem("f_attr_in")
        f_summed = sem("f_summed")
        f_relu = sem("f_relu")
        f_block = sem("f_block")
        f_picked = sem("f_picked")
        f_multiplied = sem("f_multiplied")
        f_added = sem("f_added")
        sums_done = sem("sums_done")
        y1_ready = sem("y1_ready")
        act1_ready = sem("act1_ready")
        y2_ready = sem("y2_ready")
        out_ready = sem("out_ready")
        out_stored = sem("out_stored")

        LT = 5
        LB = EG // LT
        hcopy_steps = NJ + 1

        block = ctx.enter_context(nc.Block())

        @block.sync
        def _(sp):
            def load_idx(g, s, rnd):
                if rnd is not FIRST:
                    sp.wait_ge(summed[s], rnd)
                sp.dma_start(idx[s][:, :], src_main[bass.ds(g * P, P), :]).then_inc(idx_in[s], 16)

            def load_attr(g, s, rnd):
                if rnd is not FIRST:
                    sp.wait_ge(multiplied[s], rnd)
                sp.dma_start(msg[s][:, :], e_main[bass.ds(g * P, P), :]).then_inc(attr_in[s], 16)

            def load_group(g, s, rnd):
                load_idx(g, s, rnd)
                load_attr(g, s, rnd)

            def store_block(j, ready):
                sp.wait_ge(out_ready, ready)
                sp.dma_start(out_main[:, bass.ds(j, 1), :], hm[:, bass.ds(j, 1), :]).then_inc(out_stored, 16)

            def store_tail(ready):
                sp.wait_ge(out_ready, ready)
                sp.dma_start(out[NM:N, :], out_t[0:NT, :]).then_inc(out_stored, 16)

            load_idx(0, 0, FIRST)
            for k in range(2):
                half = slice(k * NJ // 2, (k + 1) * NJ // 2)
                sp.dma_start(xm[:, half, :], x_main[:, half, :]).then_inc(half_in[k], 16)
            sp.wait_ge(xt_zeroed, 1)
            sp.dma_start(xt[0:NT, :], x[NM:N, :]).then_inc(tail_in, 16)
            for s in range(1, NS):
                load_idx(s, s, FIRST)
            for s in range(NS):
                load_attr(s, s, FIRST)
            sp.dma_start(t_msg[:, :], edge_attr[NG * GE:E, :]).then_inc(t_attr_in, 16)
            sp.dma_start(w1[:, :], W1[:, :]).then_inc(weights_in, 16)
            sp.dma_start(w2b[0:D, :], W2[:, :]).then_inc(weights_in, 16)
            sp.dma_start(w2b[D:D + 1, :], b2.rearrange("(o d) -> o d", o=1)).then_inc(weights_in, 16)
            sp.dma_start(b1c[:, :], b1.rearrange("(d o) -> d o", o=1)).then_inc(weights_in, 16)
            for k in range(2):
                half = slice(k * NJ // 2, (k + 1) * NJ // 2)
                sp.wait_ge(h_done, k + 1)
                sp.dma_start(h_rows_main[:, half, :], hm[:, half, :]).then_inc(h_stored, 16)
            sp.dma_start(h_rows[NM:N, :], ht[0:NT, :]).then_inc(h_stored, 16)

            with sp.Fori(1, LAG + 1) as i:
                for s in range(NS):
                    load_group(i * NS + s, s, i)
            with sp.Fori(LAG + 1, ROUNDS) as i:
                for s in range(NS):
                    load_group(i * NS + s, s, i)
                store_block(i - (LAG + 1), i - LAG)
            for s in range(PEELED):
                load_group(ROUNDS * NS + s, s, ROUNDS)
            sp.wait_ge(bases_ready, 1)
            is_outside = sp.value_load(outside[0:1, 0:1], min_val=0, max_val=1)
            is_redo = sp.value_load(redo[0:1, 0:1], min_val=0, max_val=1)
            for j in range(EARLY - 1, NJ):
                store_block(j, j + 1)
            store_tail(NJ + 1)

            with sp.If(is_outside == 1):
                sp.wait_ge(out_ready, NJ + 1)
                with sp.Fori(1, NG + 1) as nth:
                    rows = bass.ds((nth - 1) * P, P)
                    sp.wait_ge(f_summed, nth)
                    sp.dma_start(idx[0][:, :], src_main[rows, :]).then_inc(f_idx_in, 16)
                    sp.wait_ge(f_added, (nth - 1) * NB + 1)
                    sp.dma_start(msg[0][:, :], e_main[rows, :]).then_inc(f_attr_in, 16)
                sp.wait_ge(f_added, NG * NB + 1)
                sp.dma_start(msg[0][0:TE, 0:D], edge_attr[NG * GE:E, :]).then_inc(f_attr_in, 16)

            with sp.If(is_redo == 1):
                with sp.Fori(0, NJ) as j:
                    store_block(j, j + (NJ + 2))
                store_tail(2 * NJ + 2)
                sp.wait_ge(out_stored, 2 * 16 * (NJ + 1))
            sp.wait_ge(out_stored, 16 * (NJ + 1))

        @block.gpsimd
        def _(pool):
            nc.gpsimd.iota(node_id[:, :], pattern=[[1, WIN]], base=0, channel_multiplier=0,
                           allow_small_or_imprecise_dtypes=True).then_inc(consts, 1)
            nc.gpsimd.iota(least[:, :], pattern=[[BN, ROUNDS + 2], [0, NS]], base=-BN * LAG, channel_multiplier=0,
                           allow_small_or_imprecise_dtypes=True).then_inc(consts, 1)
            nc.gpsimd.memset(ident[:, :], 0.0).then_inc(zeroed, 1)
            pool.wait_ge(zeroed, 1)
            nc.gpsimd.affine_select(out=ident[:, :], in_=ident[:, :], compare_op=ALU.not_equal, fill=1.0,
                                    base=0, pattern=[[-1, P]], channel_multiplier=1).then_inc(consts, 1)
            def gather(idx_s, hsrc_s, done):
                for j in range(EG):
                    nc.gpsimd.indirect_dma_start(
                        out=hsrc_s[:, j * D:(j + 1) * D], out_offset=None, in_=h_rows,
                        in_offset=bass.IndirectOffsetOnAxis(ap=idx_s[:, j:j + 1], axis=0),
                    ).then_inc(done, 16)

            for s in range(NS):
                pool.wait_ge(idx_in[s], 16)
                for j in range(EG):
                    nc.gpsimd.indirect_dma_start(
                        out=hsrc[s][:, j * D:(j + 1) * D], out_offset=None, in_=x,
                        in_offset=bass.IndirectOffsetOnAxis(ap=idx[s][:, j:j + 1], axis=0),
                    ).then_inc(gathered[s], 16)
            pool.wait_ge(h_stored, 48)
            pool.wait_ge(edges_in, 48)
            nc.gpsimd.indirect_dma_start(
                out=t_hsrc[:, :], out_offset=None, in_=h_rows,
                in_offset=bass.IndirectOffsetOnAxis(ap=tail_src[:, 0:1], axis=0),
            ).then_inc(t_gathered, 16)
            with pool.Fori(2 * 16, (ROUNDS + 1) * 16, 16) as arrived:
                for s in range(NS):
                    pool.wait_ge(h_stored, 48)
                    pool.wait_ge(idx_in[s], arrived)
                    gather(idx[s], hsrc[s], gathered[s])
            for s in range(PEELED):
                pool.wait_ge(idx_in[s], (ROUNDS + 1) * 16)
                gather(idx[s], hsrc[s], gathered[s])
            pool.wait_ge(bases_ready, 1)
            with pool.If(pool.value_load(outside[0:1, 0:1], min_val=0, max_val=1) == 1):
                with pool.Fori(16, (NG + 1) * 16, 16) as arrived:
                    pool.wait_ge(h_stored, 48)
                    pool.wait_ge(f_idx_in, arrived)
                    gather(idx[0], hsrc[0], f_gathered)
                pool.wait_ge(f_summed, NG + 1)
                nc.gpsimd.indirect_dma_start(
                    out=hsrc[0][0:TE, 0:D], out_offset=None, in_=h_rows,
                    in_offset=bass.IndirectOffsetOnAxis(ap=tail_src[:, 0:1], axis=0),
                ).then_inc(f_gathered, 16)

        @block.scalar
        def _(act):
            act.dma_start(dst_row[:, :], dst_main).then_inc(edges_in, 16)
            act.dma_start(tail_src[:, :], src[NG * GE:E].rearrange("(e o) -> e o", o=1)).then_inc(edges_in, 16)
            act.dma_start(tail_dst[:, :], dst[NG * GE:E].rearrange("(o e) -> o e", o=1)).then_inc(edges_in, 16)

            for k in range(2):
                cols = slice(k * HC, NC + 1 if k else HC)
                act.wait_ge(var_done, k + 1)
                nc.scalar.activation(rstd[:, cols], var[:, cols], ACT.Sqrt, bias=eps[:, 0:1]).then_inc(std_done, 1)
            for k in range(2):
                own = range((k + 1) * NJ // 2 - AJ, (k + 1) * NJ // 2)
                act.wait_ge(scale_ready, k + 1)
                for j in own:
                    for t in range(BC):
                        c = j * BC + t
                        nc.scalar.activation(hm[:, j, t * D:(t + 1) * D], xm[:, j, t * D:(t + 1) * D], ACT.Relu,
                                             bias=shift[:, c:c + 1], scale=rstd[:, c:c + 1])
                if k:
                    nc.scalar.activation(ht[0:NT, :], xt[0:NT, :], ACT.Relu, bias=shift[0:NT, NC:NC + 1],
                                         scale=rstd[0:NT, NC:NC + 1])
                act.wait_ge(scaled, k + 1)
                rest = slice(k * NJ // 2, own[0])
                nc.scalar.activation(hm[:, rest, :], hm[:, rest, :], ACT.Relu).then_inc(h_done, 1)

            def relu(s, rnd):
                act.wait_ge(summed[s], rnd + 1)
                nc.scalar.activation(msg[s][:, :], msg[s][:, :], ACT.Relu).then_inc(relu_done[s], 1)

            def std_of_rows(s):
                act.wait_ge(e_var_done[s], 1)
                nc.scalar.activation(e_rstd[s][:, :], e_var[s][:, :], ACT.Sqrt, bias=eps[:, 0:1]
                                     ).then_inc(e_std_done[s], 1)

            std_of_rows(0)
            for j in range(NJ):
                act.wait_ge(h_tr, j + 1)
                nc.scalar.copy(sums[:, j * BN:(j + 1) * BN].rearrange("f (p t) -> f t p", t=BC),
                               tr_ps[j % 2][0:D, 0:BN].rearrange("f (t p) -> f t p", t=BC)).then_inc(h_copied, 1)
                if j == NJ // 2:
                    relu(0, FIRST)
                    std_of_rows(1)
            act.wait_ge(h_tr, NJ + 1)
            nc.scalar.copy(sums[:, NM:N], tr_ps[NJ % 2][0:D, 0:NT]).then_inc(h_copied, 1)
            relu(1, FIRST)
            for s in range(2, NS):
                std_of_rows(s)
                relu(s, FIRST)
            act.wait_ge(t_summed, 1)
            nc.scalar.activation(t_msg[:, :], t_msg[:, :], ACT.Relu).then_inc(t_relu, 1)

            def layer1(k, nth, width=BN):
                act.wait_ge(y1_ready, nth)
                nc.scalar.activation(act1[k][0:D, 0:width], tr_ps[k][0:D, 0:width], ACT.Relu, bias=b1c[:, 0:1]
                                     ).then_inc(act1_ready, 1)

            with act.Fori(1, LAG) as i:
                for s in range(NS):
                    relu(s, i)
            act.wait_ge(weights_in, 64)
            with act.Fori(LAG, ROUNDS) as i:
                for s in range(NS):
                    relu(s, i)
                layer1(0, i - (LAG - 1))
            for s in range(PEELED):
                relu(s, ROUNDS)
            act.wait_ge(bases_ready, 1)
            is_outside = act.value_load(outside[0:1, 0:1], min_val=0, max_val=1)
            is_redo = act.value_load(redo[0:1, 0:1], min_val=0, max_val=1)
            for j in range(EARLY, NJ):
                layer1(j % 2, j + 1)
            layer1(NJ % 2, NJ + 1, NT)

            with act.If(is_outside == 1):
                with act.Fori(0, NG) as g:
                    act.wait_ge(f_summed, g + 2)
                    nc.scalar.activation(msg[0][:, :], msg[0][:, :], ACT.Relu).then_inc(f_relu, 1)
                act.wait_ge(f_summed, NG + 2)
                nc.scalar.activation(msg[0][0:TE, 0:D], msg[0][0:TE, 0:D], ACT.Relu).then_inc(f_relu, 1)

            with act.If(is_redo == 1):
                with act.Fori(0, NJ // 2) as q:
                    for k in range(2):
                        layer1(k, q * 2 + (NJ + 2 + k))
                layer1(NJ % 2, 2 * NJ + 2, NT)

        @block.vector
        def _(dve):
            steps = [0]

            def then(ins):
                steps[0] += 1
                ins.then_inc(dve_prep, 1)
                dve.wait_ge(dve_prep, steps[0])

            nc.vector.memset(xt[:, :], 0.0).then_inc(xt_zeroed, 1)
            nc.vector.memset(eps[:, :], EPS).then_inc(f_summed, 1)
            nc.vector.memset(act1[0][D:D + 1, :], 1.0)
            nc.vector.memset(act1[1][D:D + 1, :], 1.0)
            nc.vector.memset(sums[:, N:N + WIN], 0.0)

            def row_variance(stats, mean, dif, var, done):
                mean_e, ssq_e, mean_o, ssq_o = (stats[:, :, k] for k in (1, 2, 4, 5))
                nc.vector.tensor_tensor(mean, mean_e, mean_o, ALU.add)
                nc.vector.tensor_tensor(dif, mean_e, mean_o, ALU.subtract)
                then(nc.vector.tensor_tensor(var, ssq_e, ssq_o, ALU.add))
                nc.vector.tensor_scalar(mean, mean, 0.5, None, ALU.mult)
                nc.vector.tensor_scalar(var, var, 1.0 / D, None, ALU.mult)
                then(nc.vector.scalar_tensor_tensor(dif, dif, 0.25, dif, ALU.mult, ALU.mult))
                nc.vector.tensor_tensor(var, var, dif, ALU.add).then_inc(done, 1)

            def row_scale(mean, rstd, shift, done):
                then(nc.vector.reciprocal(rstd, rstd))
                nc.vector.scalar_tensor_tensor(shift, mean, -1.0, rstd, ALU.mult, ALU.mult).then_inc(done, 1)

            def scale_rows(out_rows, in_rows, rstd, shift, done):
                then(nc.vector.tensor_tensor(out_rows, in_rows, rstd.unsqueeze(2).broadcast_to(in_rows.shape),
                                             ALU.mult))
                nc.vector.tensor_tensor(out_rows, out_rows, shift.unsqueeze(2).broadcast_to(in_rows.shape),
                                        ALU.add).then_inc(done, 1)

            halves = (slice(0, HC), slice(HC, NC + 1))
            column = lambda v, c: v[:, c // BC, (c % BC) * D:(c % BC + 1) * D]
            for k in range(2):
                dve.wait_ge(half_in[k], 16)
                for c in range(k * HC, (k + 1) * HC):
                    last = nc.vector.bn_stats(stats[:, c, :], column(xm, c))
                if k:
                    dve.wait_ge(tail_in, 16)
                    last = nc.vector.bn_stats(stats[:, NC, :], xt[:, :])
                last.then_inc(stats_done, 1)
                dve.wait_ge(stats_done, k + 1)
                row_variance(stats[:, halves[k], :], mean[:, halves[k]], dif[:, halves[k]], var[:, halves[k]],
                             var_done)
            for k in range(2):
                dve.wait_ge(std_done, k + 1)
                row_scale(mean[:, halves[k]], rstd[:, halves[k]], shift[:, halves[k]], scale_ready)
                j0, j1 = k * NJ // 2, (k + 1) * NJ // 2 - AJ
                rows = lambda v: v[:, j0:j1, :].rearrange("p j (t d) -> p (j t) d", t=BC)
                scale_rows(rows(hm), rows(xm), rstd[:, j0 * BC:j1 * BC], shift[:, j0 * BC:j1 * BC], scaled)

            dve.wait_ge(edges_in, 48)
            nc.vector.tensor_copy(tail_dstf[:, :], tail_dst[:, :])
            then(nc.vector.tensor_copy(dstf[:, :], dst_row[:, :]))
            nc.vector.tensor_reduce(base[:, :], dstf[:, :], AX.X, ALU.min)
            nc.vector.tensor_reduce(tail_base[:, :], tail_dstf[:, :], AX.X, ALU.min)
            nc.vector.tensor_reduce(tail_top[:, :], tail_dstf[:, :], AX.X, ALU.max)
            then(nc.vector.tensor_reduce(top[:, :], dstf[:, :], AX.X, ALU.max))
            nc.vector.tensor_scalar(rel_row[:, :], dstf[:, :], base[:, 0:1], None, ALU.subtract)
            nc.vector.tensor_copy(bases[0:1, NG:NG + 1], tail_base[:, :])
            nc.vector.tensor_tensor(spans[0:1, NG:NG + 1], tail_top[:, :], tail_base[:, :], ALU.subtract)
            nc.vector.tensor_scalar(tail_rel[:, :], tail_dstf[:, :], tail_base[:, 0:1], None, ALU.subtract)
            nc.vector.tensor_tensor(span[:, :], top[:, :], base[:, :], ALU.subtract).then_inc(rows_ready, 1)

            for k in range(LB):
                dve.wait_ge(list_tr, k + 1)
                nc.vector.tensor_copy(relT[:, :, k * LT:(k + 1) * LT],
                                      tr_ps[k % 2][:, 0:LT * NG].rearrange("p (j g) -> p g j", j=LT)
                                      ).then_inc(list_copied, 1)
            dve.wait_ge(bases_tr, 1)
            dve.wait_ge(consts, 3)
            nc.vector.tensor_copy(bases[0:1, 0:NG], y_ps[0][0:1, 0:NG])
            nc.vector.tensor_copy(spans[0:1, 0:NG], y_ps[0][0:1, P:P + NG])
            then(nc.vector.tensor_copy(tail_relT[:, :], y_ps[0][0:TE, 2 * P:2 * P + 1]))
            then(nc.vector.tensor_tensor(passed[:, :], least[:, 1:NG + 1], y_ps[0][0:1, 0:NG], ALU.subtract))
            nc.vector.tensor_reduce(widest[:, :], spans[:, :], AX.X, ALU.max)
            then(nc.vector.tensor_reduce(early[:, :], passed[:, :], AX.X, ALU.max))
            then(nc.vector.tensor_scalar(widest[:, :], widest[:, :], float(WIN), None, ALU.is_ge))
            nc.vector.tensor_copy(outside[:, :], widest[:, :])
            nc.vector.scalar_tensor_tensor(redo[:, :], early[:, :], 0.0, widest[:, :], ALU.is_gt, ALU.max
                                           ).then_inc(bases_ready, 1)

            def row_moments(s):
                dve.wait_ge(gathered[s], 16 * EG)
                for j in range(EG):
                    last = nc.vector.bn_stats(e_stats[s][:, j, :], hsrc[s][:, j * D:(j + 1) * D])
                last.then_inc(e_stats_done[s], 1)
                dve.wait_ge(e_stats_done[s], 1)
                row_variance(e_stats[s], e_mean[s][:, :], e_dif[s][:, :], e_var[s][:, :], e_var_done[s])
                dve.wait_ge(e_std_done[s], 1)
                row_scale(e_mean[s][:, :], e_rstd[s][:, :], e_shift[s][:, :], e_scale_done[s])
                rows = hsrc[s][:, :].rearrange("p (j d) -> p j d", d=D)
                scale_rows(rows, rows, e_rstd[s][:, :], e_shift[s][:, :], e_scaled[s])

            dve.wait_ge(consts, 3)
            dve.wait_ge(list_copied, LB)
            dve.wait_ge(bases_ready, 1)

            def group(g, s, rnd):
                if rnd is not FIRST:
                    dve.wait_ge(multiplied[s], rnd)
                nc.vector.tensor_tensor(
                    pick[s][:, :, :], node_id[:, :].unsqueeze(1).broadcast_to([P, EG, WIN]),
                    relT[:, bass.ds(g, 1), :].rearrange("p g j -> p (g j)").unsqueeze(2).broadcast_to([P, EG, WIN]),
                    ALU.is_equal).then_inc(picked[s], 1)
                dve.wait_ge(attr_in[s], 16 * (rnd + 1))
                if rnd is FIRST:
                    row_moments(s)
                    dve.wait_ge(e_scaled[s], 1)
                    nc.vector.scalar_tensor_tensor(msg[s][:, :], hsrc[s][:, :], 0.0, msg[s][:, :], ALU.max, ALU.add
                                                   ).then_inc(summed[s], 1)
                else:
                    dve.wait_ge(gathered[s], 16 * EG * (rnd + 1))
                    nc.vector.tensor_tensor(msg[s][:, :], msg[s][:, :], hsrc[s][:, :], ALU.add).then_inc(summed[s], 1)
                if g is not FIRST:
                    add_window(g - 1, (s - 1) % NS, rnd if s > 0 else rnd - 1)

            def add_window(g, s, rnd):
                first = dve.value_load(bases[0:1, bass.ds(g, 1)], min_val=0, max_val=N - 1)
                dve.wait_ge(multiplied[s], rnd + 1)
                if s > 0:
                    dve.wait_ge(added[s - 1], rnd + 1)
                elif rnd is not FIRST:
                    dve.wait_ge(added[NS - 1], rnd)
                else:
                    dve.wait_ge(h_copied, hcopy_steps)
                nc.vector.tensor_tensor(sums[:, bass.ds(first, WIN)], sums[:, bass.ds(first, WIN)],
                                        win_ps[s][0:D, 0:WIN], ALU.add).then_inc(added[s], 1)

            for s in range(NS):
                group(s, s, FIRST)
            nc.vector.tensor_scalar(t_pick[:, :], node_id[0:TE, :], tail_relT[:, 0:1], None, ALU.is_equal
                                    ).then_inc(t_picked, 1)
            dve.wait_ge(t_attr_in, 16)
            dve.wait_ge(t_gathered, 16)
            nc.vector.tensor_tensor(t_msg[:, :], t_msg[:, :], t_hsrc[:, :], ALU.add).then_inc(t_summed, 1)
            first = dve.value_load(bases[0:1, NG:NG + 1], min_val=0, max_val=N - 1)
            dve.wait_ge(t_multiplied, 1)
            dve.wait_ge(added[NS - 2], 1)
            nc.vector.tensor_tensor(sums[:, bass.ds(first, WIN)], sums[:, bass.ds(first, WIN)],
                                    y_ps[1][0:D, 0:WIN], ALU.add).then_inc(t_added, 1)
            nc.vector.tensor_tensor(xm[:, :, :], xm[:, :, :], hm[:, :, :], ALU.add).then_inc(xh_done, 1)
            nc.vector.tensor_tensor(xt[0:NT, :], xt[0:NT, :], ht[0:NT, :], ALU.add).then_inc(xh_done, 1)
            dve.wait_ge(t_added, 1)
            dve.wait_ge(xh_done, 2)
            dve.wait_ge(h_stored, 48)

            def finish_block(j, k, nth):
                dve.wait_ge(y2_ready, nth)
                nc.vector.scalar_tensor_tensor(
                    hm[:, bass.ds(j, 1), :].rearrange("p j d -> p (j d)"), y_ps[k][:, 0:BC * D], 0.0,
                    xm[:, bass.ds(j, 1), :].rearrange("p j d -> p (j d)"), ALU.max, ALU.add).then_inc(out_ready, 1)

            def finish_tail(nth):
                dve.wait_ge(y2_ready, nth)
                nc.vector.scalar_tensor_tensor(out_t[0:NT, :], y_ps[NJ % 2][0:NT, 0:D], 0.0, xt[0:NT, :],
                                               ALU.max, ALU.add).then_inc(out_ready, 1)

            with dve.Fori(1, LAG) as i:
                for s in range(NS):
                    group(i * NS + s, s, i)
            with dve.Fori(LAG, ROUNDS) as i:
                for s in range(NS):
                    group(i * NS + s, s, i)
                finish_block(i - LAG, 0, i - (LAG - 1))
            for s in range(PEELED):
                group(ROUNDS * NS + s, s, ROUNDS)
            add_window(NG - 1, PEELED - 1, ROUNDS)
            dve.wait_ge(bases_ready, 1)
            is_outside = dve.value_load(outside[0:1, 0:1], min_val=0, max_val=1)
            is_redo = dve.value_load(redo[0:1, 0:1], min_val=0, max_val=1)
            for j in range(EARLY, NJ):
                finish_block(j, j % 2, j + 1)
            finish_tail(NJ + 1)

            with dve.If(is_outside == 1):
                nc.vector.tensor_scalar(far_row[:, :], rel_row[:, :], float(WIN), None, ALU.is_ge)
                nc.vector.tensor_scalar(tail_far[:, :], tail_rel[:, :], float(WIN), None, ALU.is_ge)
                nc.vector.tensor_scalar(dstf[:, :], dstf[:, :], 1.0, None, ALU.add)
                then(nc.vector.tensor_scalar(tail_dstf[:, :], tail_dstf[:, :], 1.0, None, ALU.add))
                nc.vector.tensor_tensor(far_row[:, :], far_row[:, :], dstf[:, :], ALU.mult)
                then(nc.vector.tensor_tensor(tail_far[:, :], tail_far[:, :], tail_dstf[:, :], ALU.mult))
                nc.vector.tensor_scalar(far_row[:, :], far_row[:, :], -1.0, None, ALU.add)
                nc.vector.tensor_scalar(tail_far[:, :], tail_far[:, :], -1.0, None, ALU.add
                                        ).then_inc(far_rows, 1)
                nc.vector.tensor_copy(block_id[:, :], node_id[:, :]).then_inc(f_block, 1)
                nc.vector.memset(eps[:, :], EPS).then_inc(f_added, 1)
                for k in range(LB):
                    dve.wait_ge(far_tr, k + 1)
                    nc.vector.tensor_copy(relT[:, :, k * LT:(k + 1) * LT],
                                          tr_ps[k % 2][:, 0:LT * NG].rearrange("p (j g) -> p g j", j=LT)
                                          ).then_inc(far_copied, 1)
                dve.wait_ge(far_tr, LB + 1)
                nc.vector.tensor_copy(tail_relT[:, :], y_ps[0][0:TE, 0:1]).then_inc(far_copied, 1)
                dve.wait_ge(far_copied, LB + 1)

                def restart(nth):
                    dve.wait_ge(f_block, (nth - 1) * (NB + 1) + 1)
                    nc.vector.tensor_copy(block_id[:, :], node_id[:, :]).then_inc(f_block, 1)

                def add_block(nth, w, whole):
                    dve.wait_ge(f_block, (nth - 1) * (NB + 1) + w + 2)
                    if whole:
                        nc.vector.tensor_tensor(
                            pick[0][:, :, :], block_id[:, :].unsqueeze(1).broadcast_to([P, EG, WIN]),
                            relT[:, bass.ds(nth - 1, 1), :].rearrange("p g j -> p (g j)").unsqueeze(2)
                            .broadcast_to([P, EG, WIN]), ALU.is_equal).then_inc(f_picked, 1)
                    else:
                        nc.vector.tensor_scalar(pick[0][0:TE, 0, :], block_id[0:TE, :], tail_relT[:, 0:1], None,
                                                ALU.is_equal).then_inc(f_picked, 1)
                    done = (nth - 1) * NB + w + 1
                    dve.wait_ge(f_picked, done)
                    nc.vector.tensor_scalar(block_id[:, :], block_id[:, :], float(WIN), None, ALU.add
                                            ).then_inc(f_block, 1)
                    dve.wait_ge(f_multiplied, done)
                    dve.wait_ge(f_added, done)
                    nc.vector.tensor_tensor(sums[:, bass.ds(w * WIN, WIN)], sums[:, bass.ds(w * WIN, WIN)],
                                            win_ps[0][0:D, 0:WIN], ALU.add).then_inc(f_added, 1)

                with dve.Fori(1, NG + 1) as nth:
                    dve.wait_ge(f_attr_in, 16 * nth)
                    dve.wait_ge(f_gathered, 16 * EG * nth)
                    nc.vector.tensor_tensor(msg[0][:, :], msg[0][:, :], hsrc[0][:, :], ALU.add).then_inc(f_summed, 1)
                    restart(nth)
                    with dve.Fori(0, NB) as w:
                        add_block(nth, w, True)
                dve.wait_ge(f_attr_in, 16 * (NG + 1))
                dve.wait_ge(f_gathered, 16 * EG * NG + 16)
                nc.vector.tensor_tensor(msg[0][0:TE, 0:D], msg[0][0:TE, 0:D], hsrc[0][0:TE, 0:D], ALU.add
                                        ).then_inc(f_summed, 1)
                restart(NG + 1)
                with dve.Fori(0, NB) as w:
                    add_block(NG + 1, w, False)
                dve.wait_ge(f_added, (NG + 1) * NB + 1)

            with dve.If(is_redo == 1):
                dve.wait_ge(out_stored, 16 * (NJ + 1))
                nc.vector.memset(e_dif[0][:, :], 0.0).then_inc(sums_done, 1)
                with dve.Fori(0, NJ // 2) as q:
                    for k in range(2):
                        finish_block(q * 2 + k, k, q * 2 + (NJ + 2 + k))
                finish_tail(2 * NJ + 2)

        @block.tensor
        def _(pe):
            pe.wait_ge(consts, 3)
            pe.wait_ge(rows_ready, 1)
            rows = rel_row[:, :].rearrange("g (p j) -> g j p", j=EG)
            for k in range(LB):
                for t in range(LT):
                    last = nc.tensor.transpose(tr_ps[k % 2][:, t * NG:(t + 1) * NG], rows[:, k * LT + t, :],
                                               ident[0:NG, 0:NG])
                last.then_inc(list_tr, 1)
            nc.tensor.transpose(y_ps[0][0:1, 0:NG], base[:, 0:1], ident[0:NG, 0:NG])
            nc.tensor.transpose(y_ps[0][0:1, P:P + NG], span[:, 0:1], ident[0:NG, 0:NG])
            nc.tensor.transpose(y_ps[0][0:TE, 2 * P:2 * P + 1], tail_rel[:, :], ident[0:1, 0:1]
                                ).then_inc(bases_tr, 1)

            def window(s, rnd):
                pe.wait_ge(picked[s], rnd + 1)
                if rnd is not FIRST:
                    pe.wait_ge(added[s], rnd)
                pe.wait_ge(relu_done[s], rnd + 1)
                for j in range(EG):
                    last = nc.tensor.matmul(win_ps[s][0:D, 0:WIN], msg[s][:, j * D:(j + 1) * D], pick[s][:, j, :],
                                            start=(j == 0), stop=(j == EG - 1))
                last.then_inc(multiplied[s], 1)

            pe.wait_ge(list_copied, LB)
            for j in range(NJ):
                pe.wait_ge(h_done, 1 + j // (NJ // 2))
                if j >= 2:
                    pe.wait_ge(h_copied, j - 1)
                for t in range(BC):
                    last = nc.tensor.transpose(tr_ps[j % 2][0:D, t * P:(t + 1) * P], hm[:, j, t * D:(t + 1) * D],
                                               ident[:, :])
                last.then_inc(h_tr, 1)
                if j == NJ // 2:
                    window(0, FIRST)
            pe.wait_ge(h_copied, NJ - 1)
            nc.tensor.transpose(tr_ps[NJ % 2][0:D, 0:NT], ht[0:NT, :], ident[0:NT, 0:NT]).then_inc(h_tr, 1)

            for s in range(1, NS):
                window(s, FIRST)
            pe.wait_ge(t_picked, 1)
            pe.wait_ge(t_relu, 1)
            nc.tensor.matmul(y_ps[1][0:D, 0:WIN], t_msg[:, :], t_pick[:, :], start=True, stop=True
                             ).then_inc(t_multiplied, 1)

            blocks = sums[:, 0:NM].rearrange("f (j p t) -> f j t p", p=P, t=BC)

            def layer1(j, k):
                nc.tensor.matmul(tr_ps[k][0:D, 0:BN], w1[:, :],
                                 blocks[:, bass.ds(j, 1), :, :].rearrange("f j t p -> f (j t) p"),
                                 start=True, stop=True).then_inc(y1_ready, 1)

            def layer2(k, nth):
                pe.wait_ge(act1_ready, nth)
                for t in range(BC):
                    last = nc.tensor.matmul(y_ps[k][:, t * D:(t + 1) * D], act1[k][:, t * P:(t + 1) * P],
                                            w2b[:, :], start=True, stop=True)
                last.then_inc(y2_ready, 1)

            def tail_layers(nth):
                k = NJ % 2
                nc.tensor.matmul(tr_ps[k][0:D, 0:NT], w1[:, :], sums[:, NM:N], start=True, stop=True
                                 ).then_inc(y1_ready, 1)
                pe.wait_ge(act1_ready, nth)
                nc.tensor.matmul(y_ps[k][0:NT, 0:D], act1[k][:, 0:NT], w2b[:, :], start=True, stop=True
                                 ).then_inc(y2_ready, 1)

            with pe.Fori(1, LAG) as i:
                for s in range(NS):
                    window(s, i)
            pe.wait_ge(weights_in, 64)
            with pe.Fori(LAG, ROUNDS) as i:
                for s in range(NS):
                    window(s, i)
                pe.wait_ge(added[NS - 2], i + 1)
                layer1(i - LAG, 0)
                layer2(0, i - (LAG - 1))
            for s in range(PEELED):
                window(s, ROUNDS)
            pe.wait_ge(bases_ready, 1)
            is_outside = pe.value_load(outside[0:1, 0:1], min_val=0, max_val=1)
            is_redo = pe.value_load(redo[0:1, 0:1], min_val=0, max_val=1)
            pe.wait_ge(added[PEELED - 1], ROUNDS + 1)
            for j in range(EARLY, NJ):
                layer1(j, j % 2)
            for j in range(EARLY, NJ):
                layer2(j % 2, j + 1)
            pe.wait_ge(out_ready, NJ - 1)
            tail_layers(NJ + 1)

            with pe.If(is_outside == 1):
                pe.wait_ge(far_rows, 1)
                rows = far_row[:, :].rearrange("g (p j) -> g j p", j=EG)
                for k in range(LB):
                    for t in range(LT):
                        last = nc.tensor.transpose(tr_ps[k % 2][:, t * NG:(t + 1) * NG], rows[:, k * LT + t, :],
                                                   ident[0:NG, 0:NG])
                    last.then_inc(far_tr, 1)
                nc.tensor.transpose(y_ps[0][0:TE, 0:1], tail_far[:, :], ident[0:1, 0:1]).then_inc(far_tr, 1)
                pe.wait_ge(far_copied, LB + 1)
                with pe.Fori(1, NG + 1) as nth:
                    pe.wait_ge(far_rows, 1)
                    pe.wait_ge(f_relu, nth)
                    with pe.Fori(0, NB) as w:
                        pe.wait_ge(f_picked, (nth - 1) * NB + w + 1)
                        pe.wait_ge(f_added, (nth - 1) * NB + w + 1)
                        for j in range(EG):
                            last = nc.tensor.matmul(win_ps[0][0:D, 0:WIN], msg[0][:, j * D:(j + 1) * D],
                                                    pick[0][:, j, :], start=(j == 0), stop=(j == EG - 1))
                        last.then_inc(f_multiplied, 1)
                pe.wait_ge(f_relu, NG + 1)
                with pe.Fori(0, NB) as w:
                    pe.wait_ge(f_picked, NG * NB + w + 1)
                    pe.wait_ge(f_added, NG * NB + w + 1)
                    nc.tensor.matmul(win_ps[0][0:D, 0:WIN], msg[0][0:TE, 0:D], pick[0][0:TE, 0, :],
                                     start=True, stop=True).then_inc(f_multiplied, 1)

            with pe.If(is_redo == 1):
                pe.wait_ge(sums_done, 1)
                with pe.Fori(0, NJ // 2) as q:
                    for k in range(2):
                        layer1(q * 2 + k, k)
                    pe.wait_ge(out_ready, q * 2 + (NJ + 1))
                    for k in range(2):
                        layer2(k, q * 2 + (NJ + 2 + k))
                pe.wait_ge(out_ready, 2 * NJ + 1)
                tail_layers(2 * NJ + 2)


_INS = ["x", "src", "dst", "edge_attr_96", "L0_gnn_W1", "L0_gnn_b1", "L0_gnn_W2", "L0_gnn_b2"]


def kernel(**inputs):
    import numpy as _np
    import concourse.bacc as _bacc
    from concourse.bass_utils import run_bass_kernel_spmd as _run

    nc = _bacc.Bacc("TRN2", target_bir_lowering=False, num_devices=1)
    arrays, args = {}, []
    for name in _INS:
        a = _np.ascontiguousarray(inputs[name])
        arrays[name] = a
        args.append(nc.dram_tensor(name, a.shape, mybir.dt.from_np(a.dtype), kind="ExternalInput").ap())
    args.append(nc.dram_tensor("out", arrays["x"].shape, F32, kind="ExternalOutput").ap())
    gnn_kernel(nc, *args)
    r = _run(nc, [arrays], core_ids=[0])
    return r.results[0]["out"]
```

```python
from contextlib import ExitStack

import concourse.bass as bass
from concourse import mybir

F32 = mybir.dt.float32
I32 = mybir.dt.int32
BF16 = mybir.dt.bfloat16
ALU = mybir.AluOpType
ACT = mybir.ActivationFunctionType
AX = mybir.AxisListType


def gnn_kernel(nc, x, src, dst, edge_attr, W1, b1, W2, b2, out):
    N, D = x.shape
    E = src.shape[0]
    P = 128
    EPS = 1e-5

    EG = 10
    GE = EG * P
    PG = EG - 1
    GPE = PG * P
    NG = E // GE
    TE = E - NG * GE
    assert 0 < TE <= P and NG <= P and TE <= EG
    WIN = 96
    NS = 4
    FIRST = 0
    ROUNDS = (NG - 1) // NS
    PEELED = NG - ROUNDS * NS
    assert 1 < PEELED < NS
    FR = 2
    FG = FR * NS

    BC = 3
    BN = BC * P
    NJ = N // BN
    NC = NJ * BC
    NM = NJ * BN
    NT = N - NM
    HC = NC // 2
    NB = -(-N // WIN)
    FB = 2
    LAG = 5
    EARLY = ROUNDS - LAG
    AJ = 2
    assert NM + P == P * (-(-N // P))
    assert 0 < NT <= P and NJ % 2 == 0 and EARLY < NJ

    TK = -(-N // P)
    TA = (TK + 1) // 2
    batches = ((0, TA), (TA, TK))
    PARTS = 3
    last_steps = ((0, EG - 3), (EG - 3, EG))

    e_groups = edge_attr[0:NG * GE, :].rearrange("(g e) d -> g e d", e=GE)
    e_main = e_groups[:, 0:GPE, :].rearrange("g (p j) d -> p g (j d)", j=PG)
    e_last = e_groups[:, GPE:GE, :].rearrange("g p d -> p g d")
    x_main = x[0:NM, :].rearrange("(j p t) d -> p j (t d)", p=P, t=BC)
    out_main = out[0:NM, :].rearrange("(j p t) d -> p j (t d)", p=P, t=BC)
    src_groups = src[0:NG * GE].rearrange("(g e) -> g e", e=GE)
    src_main = src_groups[:, 0:GPE].rearrange("g (p j) -> p g j", j=PG)
    src_last = src_groups[:, GPE:GE].rearrange("g (p o) -> p g o", o=1)
    dst_main = dst[0:NG * GE].rearrange("(g e) -> g e", e=GE)

    with ExitStack() as ctx:
        def sb(name, shape, dt=F32):
            return ctx.enter_context(nc.sbuf_tensor(name, shape, dt))

        def ps(name, shape):
            return ctx.enter_context(nc.psum_tensor(name, shape, F32))

        def sem(name):
            return ctx.enter_context(nc.semaphore(name))

        def sems(name):
            return [sem(f"{name}{s}") for s in range(NS)]

        h_rows = nc.dram_tensor("h_rows", (P * TK, D), F32, kind="Internal").ap()
        h_table = h_rows.rearrange("(p k) d -> p (k d)", k=TK)
        h_rows_main = h_rows[0:NM, :].rearrange("(j p t) d -> p j (t d)", p=P, t=BC)

        xm = sb("xm", [P, NJ, BC * D])
        xt = sb("xt", [P, D])
        hm = sb("hm", [P, NJ, BC * D])
        ht = sb("ht", [P, D])
        stats = sb("stats", [P, NC + 1, 6])
        mean = sb("mean", [P, NC + 1])
        var = sb("var", [P, NC + 1])
        dif = sb("dif", [P, NC + 1])
        rstd = sb("rstd", [P, NC + 1])
        shift = sb("shift", [P, NC + 1])
        eps = sb("eps", [P, 1])
        sums = sb("sums", [D, N + WIN])
        w1 = sb("w1", [D, D])
        w2b = sb("w2b", [D + 1, D])
        b1c = sb("b1c", [D, 1])
        act1 = [sb(f"act1_{k}", [D + 1, BN]) for k in range(2)]
        out_t = sb("out_t", [P, D])
        ident = sb("ident", [P, P])
        dst_row = sb("dst_row", [NG, GE], I32)
        dstf = sb("dstf", [NG, GE])
        rel_row = sb("rel_row", [NG, GE])
        far_row = sb("far_row", [NG, GE])
        base = sb("base", [NG, 1])
        top = sb("top", [NG, 1])
        span = sb("span", [NG, 1])
        relT = sb("relT", [P, NG, EG])
        tail_src = sb("tail_src", [TE, 1], I32)
        tail_dst = sb("tail_dst", [1, TE], I32)
        tail_dstf = sb("tail_dstf", [1, TE])
        tail_rel = sb("tail_rel", [1, TE])
        tail_far = sb("tail_far", [1, TE])
        tail_relT = sb("tail_relT", [TE, 1])
        tail_base = sb("tail_base", [1, 1])
        tail_top = sb("tail_top", [1, 1])
        spans = sb("spans", [1, NG + 1])
        widest = sb("widest", [1, 1])
        outside = sb("outside", [1, 1], I32)
        least = sb("least", [1, (ROUNDS + 2) * NS])
        passed = sb("passed", [1, NG])
        early = sb("early", [1, 1])
        redo = sb("redo", [1, 1], I32)
        bases = sb("bases", [1, NG + 1], I32)
        node_id = sb("node_id", [P, WIN])
        block_id = sb("block_id", [P, WIN])
        table = sb("table", [P, TK, PARTS, D], BF16)
        row0 = sb("row0", [P, 1])
        col_id = sb("col_id", [P, TK])
        col_ids = sb("col_ids", [P, TK, P], BF16)
        src_all = [sb(f"src_all{s}", [P, P], I32) for s in range(NS)]
        src_off = sb("src_off", [P, P], BF16)
        choose = sb("choose", [P, TK, P], BF16)
        h_wave = choose[:, :, :].rearrange("p k e -> p (k e)")[:, 0:TA * D * 2].bitcast(F32)
        idx = [sb(f"idx{s}", [P, EG], I32) for s in range(NS)]
        hsrc = [sb(f"hsrc{s}", [P, EG * D]) for s in range(NS)]
        msg = [sb(f"msg{s}", [P, EG * D]) for s in range(NS)]
        t_hsrc = sb("t_hsrc", [TE, D])
        t_msg = sb("t_msg", [TE, D])
        t_pick = sb("t_pick", [TE, WIN])
        e_stats = [sb(f"e_stats{s}", [P, EG, 6]) for s in range(NS)]
        e_mean = [sb(f"e_mean{s}", [P, EG]) for s in range(NS)]
        e_var = [sb(f"e_var{s}", [P, EG]) for s in range(NS)]
        e_dif = [sb(f"e_dif{s}", [P, EG]) for s in range(NS)]
        e_rstd = [sb(f"e_rstd{s}", [P, EG]) for s in range(NS)]
        e_shift = [sb(f"e_shift{s}", [P, EG]) for s in range(NS)]
        pick = [sb(f"pick{s}", [P, EG, WIN]) for s in range(NS)]

        win_ps = [ps(f"win_ps{k}", [P, 512]) for k in range(2)]
        row_ps = [ps(f"row_ps{k}", [P, 512]) for k in range(2)]
        tr_ps = [ps(f"tr_ps{k}", [P, 512]) for k in range(2)]
        y_ps = [ps(f"y_ps{k}", [P, 512]) for k in range(2)]

        edges_in = sem("edges_in")
        half_in = [sem(f"half_in{k}") for k in range(2)]
        tail_in = sem("tail_in")
        weights_in = sem("weights_in")
        consts = sem("consts")
        zeroed = sem("zeroed")
        dve_prep = sem("dve_prep")
        xt_zeroed = sem("xt_zeroed")
        stats_done = sem("stats_done")
        var_done = sem("var_done")
        std_done = sem("std_done")
        scale_ready = sem("scale_ready")
        scaled = sem("scaled")
        h_done = sem("h_done")
        h_stored = sem("h_stored")
        xh_done = sem("xh_done")
        rows_ready = sem("rows_ready")
        list_tr = sem("list_tr")
        list_copied = sem("list_copied")
        bases_tr = sem("bases_tr")
        bases_ready = sem("bases_ready")
        h_tr = sem("h_tr")
        h_copied = sem("h_copied")
        idx_in = sems("idx_in")
        e_stats_done = sems("e_stats_done")
        e_var_done = sems("e_var_done")
        e_std_done = sems("e_std_done")
        e_scale_done = sems("e_scale_done")
        e_scaled = sems("e_scaled")
        gathered = sems("gathered")
        last_gathered = sem("last_gathered")
        attr_in = sems("attr_in")
        summed = sems("summed")
        relu_done = sems("relu_done")
        picked = sems("picked")
        multiplied = sems("multiplied")
        added = sems("added")
        wave_in = sem("wave_in")
        wave_hi = sem("wave_hi")
        wave_rest = sem("wave_rest")
        wave_mid = sem("wave_mid")
        wave_lo = sem("wave_lo")
        col_ids_ready = sem("col_ids_ready")
        src_all_in = sems("src_all_in")
        src_off_ready = sem("src_off_ready")
        chosen = [sem(f"chosen{b}") for b in range(2)]
        fetched = [sem(f"fetched{b}") for b in range(2)]
        rows_summed = sem("rows_summed")
        t_attr_in = sem("t_attr_in")
        t_gathered = sem("t_gathered")
        t_summed = sem("t_summed")
        t_relu = sem("t_relu")
        t_picked = sem("t_picked")
        t_multiplied = sem("t_multiplied")
        t_added = sem("t_added")
        far_rows = sem("far_rows")
        far_tr = sem("far_tr")
        far_copied = sem("far_copied")
        f_idx_in = sem("f_idx_in")
        f_gathered = sem("f_gathered")
        f_attr_in = sem("f_attr_in")
        f_summed = sem("f_summed")
        f_relu = sem("f_relu")
        f_block = sem("f_block")
        f_picked = sem("f_picked")
        f_multiplied = sem("f_multiplied")
        f_added = sem("f_added")
        sums_done = sem("sums_done")
        y1_ready = sem("y1_ready")
        act1_ready = sem("act1_ready")
        y2_ready = sem("y2_ready")
        out_ready = sem("out_ready")
        out_stored = sem("out_stored")

        LT = 5
        LB = EG // LT
        hcopy_steps = NJ + 1

        block = ctx.enter_context(nc.Block())

        @block.sync
        def _(sp):
            def load_idx(g, s, rnd):
                if rnd is not FIRST:
                    sp.wait_ge(summed[s], rnd)
                sp.dma_start(idx[s][:, 0:PG], src_main[:, bass.ds(g, 1), :]).then_inc(idx_in[s], 16)
                if isinstance(g, int) and g < FG:
                    sp.dma_start(idx[s][:, PG:EG], src_last[:, g, :]).then_inc(idx_in[s], 16)

            def load_src_all(g, s):
                sp.dma_start(src_all[s][:, :], src_groups[bass.ds(g, 1), GPE:GE].broadcast_to([P, P])
                             ).then_inc(src_all_in[s], 16)

            def load_attr(g, s, rnd):
                if rnd is not FIRST:
                    sp.wait_ge(multiplied[s], rnd)
                sp.dma_start(msg[s][:, 0:PG * D], e_main[:, bass.ds(g, 1), :]).then_inc(attr_in[s], 16)
                sp.dma_start(msg[s][:, PG * D:EG * D], e_last[:, bass.ds(g, 1), :]).then_inc(attr_in[s], 16)

            def load_group(g, s, rnd):
                load_idx(g, s, rnd)
                if not isinstance(g, int) or g >= FG:
                    load_src_all(g, s)
                load_attr(g, s, rnd)

            def store_block(j, ready):
                sp.wait_ge(out_ready, ready)
                sp.dma_start(out_main[:, bass.ds(j, 1), :], hm[:, bass.ds(j, 1), :]).then_inc(out_stored, 16)

            def store_tail(ready):
                sp.wait_ge(out_ready, ready)
                sp.dma_start(out[NM:N, :], out_t[0:NT, :]).then_inc(out_stored, 16)

            load_idx(0, 0, FIRST)
            for k in range(2):
                half = slice(k * NJ // 2, (k + 1) * NJ // 2)
                sp.dma_start(xm[:, half, :], x_main[:, half, :]).then_inc(half_in[k], 16)
            sp.wait_ge(xt_zeroed, 1)
            sp.dma_start(xt[0:NT, :], x[NM:N, :]).then_inc(tail_in, 16)
            for s in range(1, NS):
                load_idx(s, s, FIRST)
            for s in range(NS):
                load_attr(s, s, FIRST)
            sp.dma_start(t_msg[:, :], edge_attr[NG * GE:E, :]).then_inc(t_attr_in, 16)
            sp.dma_start(w1[:, :], W1[:, :]).then_inc(weights_in, 16)
            sp.dma_start(w2b[0:D, :], W2[:, :]).then_inc(weights_in, 16)
            sp.dma_start(w2b[D:D + 1, :], b2.rearrange("(o d) -> o d", o=1)).then_inc(weights_in, 16)
            sp.dma_start(b1c[:, :], b1.rearrange("(d o) -> d o", o=1)).then_inc(weights_in, 16)
            for k in range(2):
                half = slice(k * NJ // 2, (k + 1) * NJ // 2)
                sp.wait_ge(h_done, k + 1)
                sp.dma_start(h_rows_main[:, half, :], hm[:, half, :]).then_inc(h_stored, 16)
            sp.dma_start(h_rows[NM:NM + P, :], ht[:, :]).then_inc(h_stored, 16)
            sp.wait_ge(h_stored, 48)
            sp.dma_start(h_wave[:, 0:TA * D], h_table[:, 0:TA * D]).then_inc(wave_in, 16)

            for s in range(NS):
                load_group(NS + s, s, 1)
                if s == NS - 1:
                    sp.wait_ge(wave_lo, 1)
                    sp.dma_start(h_wave[:, 0:(TK - TA) * D], h_table[:, TA * D:TK * D]).then_inc(wave_in, 16)
            with sp.Fori(2, LAG + 1) as i:
                for s in range(NS):
                    load_group(i * NS + s, s, i)
            with sp.Fori(LAG + 1, ROUNDS) as i:
                for s in range(NS):
                    load_group(i * NS + s, s, i)
                store_block(i - (LAG + 1), i - LAG)
            for s in range(PEELED):
                load_group(ROUNDS * NS + s, s, ROUNDS)
            sp.wait_ge(bases_ready, 1)
            is_outside = sp.value_load(outside[0:1, 0:1], min_val=0, max_val=1)
            is_redo = sp.value_load(redo[0:1, 0:1], min_val=0, max_val=1)
            for j in range(EARLY - 1, NJ):
                store_block(j, j + 1)
            store_tail(NJ + 1)

            with sp.If(is_outside == 1):
                sp.wait_ge(out_ready, NJ + 1)
                with sp.Fori(1, NG + 1) as nth:
                    g = bass.ds(nth - 1, 1)
                    sp.wait_ge(f_summed, nth)
                    sp.dma_start(idx[0][:, 0:PG], src_main[:, g, :]).then_inc(f_idx_in, 16)
                    sp.dma_start(idx[0][:, PG:EG], src_last[:, g, :]).then_inc(f_idx_in, 16)
                    sp.wait_ge(f_added, (nth - 1) * NB + 1)
                    sp.dma_start(msg[0][:, 0:PG * D], e_main[:, g, :]).then_inc(f_attr_in, 16)
                    sp.dma_start(msg[0][:, PG * D:EG * D], e_last[:, g, :]).then_inc(f_attr_in, 16)
                sp.wait_ge(f_added, NG * NB + 1)
                sp.dma_start(msg[0][0:TE, 0:D], edge_attr[NG * GE:E, :]).then_inc(f_attr_in, 16)

            with sp.If(is_redo == 1):
                with sp.Fori(0, NJ) as j:
                    store_block(j, j + (NJ + 2))
                store_tail(2 * NJ + 2)
                sp.wait_ge(out_stored, 2 * 16 * (NJ + 1))
            sp.wait_ge(out_stored, 16 * (NJ + 1))

        @block.gpsimd
        def _(pool):
            nc.gpsimd.iota(node_id[:, :], pattern=[[1, WIN]], base=0, channel_multiplier=0,
                           allow_small_or_imprecise_dtypes=True).then_inc(consts, 1)
            nc.gpsimd.iota(least[:, :], pattern=[[BN, ROUNDS + 2], [0, NS]], base=-BN * LAG, channel_multiplier=0,
                           allow_small_or_imprecise_dtypes=True).then_inc(consts, 1)
            nc.gpsimd.iota(row0[:, :], pattern=[[0, 1]], base=0, channel_multiplier=TK,
                           allow_small_or_imprecise_dtypes=True).then_inc(consts, 1)
            nc.gpsimd.iota(col_id[:, :], pattern=[[1, TK]], base=0, channel_multiplier=0,
                           allow_small_or_imprecise_dtypes=True).then_inc(consts, 1)
            nc.gpsimd.memset(ident[:, :], 0.0).then_inc(zeroed, 1)
            pool.wait_ge(zeroed, 1)
            nc.gpsimd.affine_select(out=ident[:, :], in_=ident[:, :], compare_op=ALU.not_equal, fill=1.0,
                                    base=0, pattern=[[-1, P]], channel_multiplier=1).then_inc(consts, 1)
            def gather(idx_s, hsrc_s, done, tiles):
                for j in tiles:
                    nc.gpsimd.indirect_dma_start(
                        out=hsrc_s[:, j * D:(j + 1) * D], out_offset=None, in_=h_rows,
                        in_offset=bass.IndirectOffsetOnAxis(ap=idx_s[:, j:j + 1], axis=0),
                    ).then_inc(done, 16)

            for s in range(NS):
                pool.wait_ge(idx_in[s], 2 * 16)
                for j in range(EG):
                    nc.gpsimd.indirect_dma_start(
                        out=hsrc[s][:, j * D:(j + 1) * D], out_offset=None, in_=x,
                        in_offset=bass.IndirectOffsetOnAxis(ap=idx[s][:, j:j + 1], axis=0),
                    ).then_inc(gathered[s], 16)
            pool.wait_ge(h_stored, 48)
            pool.wait_ge(edges_in, 48)
            nc.gpsimd.indirect_dma_start(
                out=t_hsrc[:, :], out_offset=None, in_=h_rows,
                in_offset=bass.IndirectOffsetOnAxis(ap=tail_src[:, 0:1], axis=0),
            ).then_inc(t_gathered, 16)
            for s in range(NS):
                pool.wait_ge(idx_in[s], 4 * 16)
                gather(idx[s], hsrc[s], gathered[s], range(EG))
            with pool.Fori((2 * FR + 1) * 16, (ROUNDS + FR + 1) * 16, 16) as arrived:
                for s in range(NS):
                    pool.wait_ge(h_stored, 48)
                    pool.wait_ge(idx_in[s], arrived)
                    gather(idx[s], hsrc[s], gathered[s], range(PG))
            for s in range(PEELED):
                pool.wait_ge(idx_in[s], (ROUNDS + FR + 1) * 16)
                before = last_steps[0][1] if s == PEELED - 1 else PG
                gather(idx[s], hsrc[s], gathered[s], range(before))
                gather(idx[s], hsrc[s], last_gathered, range(before, PG))
            pool.wait_ge(bases_ready, 1)
            with pool.If(pool.value_load(outside[0:1, 0:1], min_val=0, max_val=1) == 1):
                with pool.Fori(2 * 16, (NG + 1) * 2 * 16, 2 * 16) as arrived:
                    pool.wait_ge(h_stored, 48)
                    pool.wait_ge(f_idx_in, arrived)
                    gather(idx[0], hsrc[0], f_gathered, range(EG))
                pool.wait_ge(f_summed, NG + 1)
                nc.gpsimd.indirect_dma_start(
                    out=hsrc[0][0:TE, 0:D], out_offset=None, in_=h_rows,
                    in_offset=bass.IndirectOffsetOnAxis(ap=tail_src[:, 0:1], axis=0),
                ).then_inc(f_gathered, 16)

        @block.scalar
        def _(act):
            act.dma_start(dst_row[:, :], dst_main).then_inc(edges_in, 16)
            act.dma_start(tail_src[:, :], src[NG * GE:E].rearrange("(e o) -> e o", o=1)).then_inc(edges_in, 16)
            act.dma_start(tail_dst[:, :], dst[NG * GE:E].rearrange("(o e) -> o e", o=1)).then_inc(edges_in, 16)

            act.wait_ge(consts, 5)
            nc.scalar.copy(col_ids[:, :, :], col_id[:, :].unsqueeze(2).broadcast_to([P, TK, P])
                           ).then_inc(col_ids_ready, 1)

            for k in range(2):
                cols = slice(k * HC, NC + 1 if k else HC)
                act.wait_ge(var_done, k + 1)
                nc.scalar.activation(rstd[:, cols], var[:, cols], ACT.Sqrt, bias=eps[:, 0:1]).then_inc(std_done, 1)
            for k in range(2):
                own = range((k + 1) * NJ // 2 - AJ, (k + 1) * NJ // 2)
                act.wait_ge(scale_ready, k + 1)
                for j in own:
                    for t in range(BC):
                        c = j * BC + t
                        nc.scalar.activation(hm[:, j, t * D:(t + 1) * D], xm[:, j, t * D:(t + 1) * D], ACT.Relu,
                                             bias=shift[:, c:c + 1], scale=rstd[:, c:c + 1])
                if k:
                    nc.scalar.activation(ht[:, :], xt[:, :], ACT.Relu, bias=shift[:, NC:NC + 1],
                                         scale=rstd[:, NC:NC + 1])
                act.wait_ge(scaled, k + 1)
                rest = slice(k * NJ // 2, own[0])
                nc.scalar.activation(hm[:, rest, :], hm[:, rest, :], ACT.Relu).then_inc(h_done, 1)

            def relu(s, rnd):
                act.wait_ge(summed[s], rnd + 1)
                nc.scalar.activation(msg[s][:, :], msg[s][:, :], ACT.Relu).then_inc(relu_done[s], 1)

            def std_of_rows(s):
                act.wait_ge(e_var_done[s], 1)
                nc.scalar.activation(e_rstd[s][:, :], e_var[s][:, :], ACT.Sqrt, bias=eps[:, 0:1]
                                     ).then_inc(e_std_done[s], 1)

            def wave(b):
                k0, k1 = batches[b]
                return h_wave[:, 0:(k1 - k0) * D].rearrange("p (k d) -> p k d", d=D), slice(k0, k1)

            def high_part(b):
                act.wait_ge(wave_in, 16 * (b + 1))
                h, cols = wave(b)
                nc.scalar.copy(table[:, cols, 0, :], h).then_inc(wave_hi, 1)

            def middle_part(b):
                act.wait_ge(wave_rest, b + 1)
                h, cols = wave(b)
                nc.scalar.copy(table[:, cols, 1, :], h).then_inc(wave_mid, 1)

            std_of_rows(0)
            for j in range(NJ):
                act.wait_ge(h_tr, j + 1)
                nc.scalar.copy(sums[:, j * BN:(j + 1) * BN].rearrange("f (p t) -> f t p", t=BC),
                               tr_ps[j % 2][0:D, 0:BN].rearrange("f (t p) -> f t p", t=BC)).then_inc(h_copied, 1)
                if j == NJ // 2:
                    relu(0, FIRST)
                if j == NJ // 2 + 3:
                    std_of_rows(1)
            act.wait_ge(h_tr, NJ + 1)
            nc.scalar.copy(sums[:, NM:N], tr_ps[NJ % 2][0:D, 0:NT]).then_inc(h_copied, 1)
            relu(1, FIRST)
            std_of_rows(2)
            relu(2, FIRST)
            high_part(0)
            std_of_rows(3)
            relu(3, FIRST)
            middle_part(0)
            act.wait_ge(t_summed, 1)
            nc.scalar.activation(t_msg[:, :], t_msg[:, :], ACT.Relu).then_inc(t_relu, 1)

            def layer1(k, nth, width=BN):
                act.wait_ge(y1_ready, nth)
                nc.scalar.activation(act1[k][0:D, 0:width], tr_ps[k][0:D, 0:width], ACT.Relu, bias=b1c[:, 0:1]
                                     ).then_inc(act1_ready, 1)

            relu(0, 1)
            relu(1, 1)
            high_part(1)
            relu(2, 1)
            middle_part(1)
            relu(3, 1)
            with act.Fori(FR, LAG) as i:
                for s in range(NS):
                    relu(s, i)
            act.wait_ge(weights_in, 64)
            with act.Fori(LAG, ROUNDS) as i:
                for s in range(FB + 1):
                    relu(s, i)
                layer1(0, i - (LAG - 1))
                for s in range(FB + 1, NS):
                    relu(s, i)
            for s in range(PEELED - 1):
                relu(s, ROUNDS)
            for n, (j0, j1) in enumerate(last_steps):
                act.wait_ge(summed[PEELED - 1], ROUNDS + 1 + n)
                nc.scalar.activation(msg[PEELED - 1][:, j0 * D:j1 * D], msg[PEELED - 1][:, j0 * D:j1 * D], ACT.Relu
                                     ).then_inc(relu_done[PEELED - 1], 1)
            act.wait_ge(bases_ready, 1)
            is_outside = act.value_load(outside[0:1, 0:1], min_val=0, max_val=1)
            is_redo = act.value_load(redo[0:1, 0:1], min_val=0, max_val=1)
            for j in range(EARLY, NJ):
                layer1(j % 2, j + 1)
            layer1(NJ % 2, NJ + 1, NT)

            with act.If(is_outside == 1):
                with act.Fori(0, NG) as g:
                    act.wait_ge(f_summed, g + 2)
                    nc.scalar.activation(msg[0][:, :], msg[0][:, :], ACT.Relu).then_inc(f_relu, 1)
                act.wait_ge(f_summed, NG + 2)
                nc.scalar.activation(msg[0][0:TE, 0:D], msg[0][0:TE, 0:D], ACT.Relu).then_inc(f_relu, 1)

            with act.If(is_redo == 1):
                with act.Fori(0, NJ // 2) as q:
                    for k in range(2):
                        layer1(k, q * 2 + (NJ + 2 + k))
                layer1(NJ % 2, 2 * NJ + 2, NT)

        @block.vector
        def _(dve):
            steps = [0]

            def then(ins):
                steps[0] += 1
                ins.then_inc(dve_prep, 1)
                dve.wait_ge(dve_prep, steps[0])

            nc.vector.memset(xt[:, :], 0.0).then_inc(xt_zeroed, 1)
            nc.vector.memset(eps[:, :], EPS).then_inc(f_summed, 1)
            nc.vector.memset(act1[0][D:D + 1, :], 1.0)
            nc.vector.memset(act1[1][D:D + 1, :], 1.0)
            nc.vector.memset(sums[:, N:N + WIN], 0.0)

            def row_variance(stats, mean, dif, var, done):
                mean_e, ssq_e, mean_o, ssq_o = (stats[:, :, k] for k in (1, 2, 4, 5))
                nc.vector.tensor_tensor(mean, mean_e, mean_o, ALU.add)
                nc.vector.tensor_tensor(dif, mean_e, mean_o, ALU.subtract)
                then(nc.vector.tensor_tensor(var, ssq_e, ssq_o, ALU.add))
                nc.vector.tensor_scalar(mean, mean, 0.5, None, ALU.mult)
                nc.vector.tensor_scalar(var, var, 1.0 / D, None, ALU.mult)
                then(nc.vector.scalar_tensor_tensor(dif, dif, 0.25, dif, ALU.mult, ALU.mult))
                nc.vector.tensor_tensor(var, var, dif, ALU.add).then_inc(done, 1)

            def row_scale(mean, rstd, shift, done):
                then(nc.vector.reciprocal(rstd, rstd))
                nc.vector.scalar_tensor_tensor(shift, mean, -1.0, rstd, ALU.mult, ALU.mult).then_inc(done, 1)

            def scale_rows(out_rows, in_rows, rstd, shift, done):
                then(nc.vector.tensor_tensor(out_rows, in_rows, rstd.unsqueeze(2).broadcast_to(in_rows.shape),
                                             ALU.mult))
                nc.vector.tensor_tensor(out_rows, out_rows, shift.unsqueeze(2).broadcast_to(in_rows.shape),
                                        ALU.add).then_inc(done, 1)

            halves = (slice(0, HC), slice(HC, NC + 1))
            column = lambda v, c: v[:, c // BC, (c % BC) * D:(c % BC + 1) * D]
            for k in range(2):
                dve.wait_ge(half_in[k], 16)
                for c in range(k * HC, (k + 1) * HC):
                    last = nc.vector.bn_stats(stats[:, c, :], column(xm, c))
                if k:
                    dve.wait_ge(tail_in, 16)
                    last = nc.vector.bn_stats(stats[:, NC, :], xt[:, :])
                last.then_inc(stats_done, 1)
                dve.wait_ge(stats_done, k + 1)
                row_variance(stats[:, halves[k], :], mean[:, halves[k]], dif[:, halves[k]], var[:, halves[k]],
                             var_done)
            for k in range(2):
                dve.wait_ge(std_done, k + 1)
                row_scale(mean[:, halves[k]], rstd[:, halves[k]], shift[:, halves[k]], scale_ready)
                j0, j1 = k * NJ // 2, (k + 1) * NJ // 2 - AJ
                rows = lambda v: v[:, j0:j1, :].rearrange("p j (t d) -> p (j t) d", t=BC)
                scale_rows(rows(hm), rows(xm), rstd[:, j0 * BC:j1 * BC], shift[:, j0 * BC:j1 * BC], scaled)

            dve.wait_ge(edges_in, 48)
            nc.vector.tensor_copy(tail_dstf[:, :], tail_dst[:, :])
            then(nc.vector.tensor_copy(dstf[:, :], dst_row[:, :]))
            nc.vector.tensor_reduce(base[:, :], dstf[:, :], AX.X, ALU.min)
            nc.vector.tensor_reduce(tail_base[:, :], tail_dstf[:, :], AX.X, ALU.min)
            nc.vector.tensor_reduce(tail_top[:, :], tail_dstf[:, :], AX.X, ALU.max)
            then(nc.vector.tensor_reduce(top[:, :], dstf[:, :], AX.X, ALU.max))
            nc.vector.tensor_scalar(rel_row[:, :], dstf[:, :], base[:, 0:1], None, ALU.subtract)
            nc.vector.tensor_copy(bases[0:1, NG:NG + 1], tail_base[:, :])
            nc.vector.tensor_tensor(spans[0:1, NG:NG + 1], tail_top[:, :], tail_base[:, :], ALU.subtract)
            nc.vector.tensor_scalar(tail_rel[:, :], tail_dstf[:, :], tail_base[:, 0:1], None, ALU.subtract)
            nc.vector.tensor_tensor(span[:, :], top[:, :], base[:, :], ALU.subtract).then_inc(rows_ready, 1)

            for k in range(LB):
                dve.wait_ge(list_tr, k + 1)
                nc.vector.tensor_copy(relT[:, :, k * LT:(k + 1) * LT],
                                      tr_ps[k % 2][:, 0:LT * NG].rearrange("p (j g) -> p g j", j=LT)
                                      ).then_inc(list_copied, 1)
            dve.wait_ge(bases_tr, 1)
            dve.wait_ge(consts, 5)
            nc.vector.tensor_copy(bases[0:1, 0:NG], y_ps[0][0:1, 0:NG])
            nc.vector.tensor_copy(spans[0:1, 0:NG], y_ps[0][0:1, P:P + NG])
            then(nc.vector.tensor_copy(tail_relT[:, :], y_ps[0][0:TE, 2 * P:2 * P + 1]))
            then(nc.vector.tensor_tensor(passed[:, :], least[:, FB:NG + FB], y_ps[0][0:1, 0:NG], ALU.subtract))
            nc.vector.tensor_reduce(widest[:, :], spans[:, :], AX.X, ALU.max)
            then(nc.vector.tensor_reduce(early[:, :], passed[:, :], AX.X, ALU.max))
            then(nc.vector.tensor_scalar(widest[:, :], widest[:, :], float(WIN), None, ALU.is_ge))
            nc.vector.tensor_copy(outside[:, :], widest[:, :])
            nc.vector.scalar_tensor_tensor(redo[:, :], early[:, :], 0.0, widest[:, :], ALU.is_gt, ALU.max
                                           ).then_inc(bases_ready, 1)

            def row_moments(s):
                dve.wait_ge(gathered[s], 16 * EG)
                for j in range(EG):
                    last = nc.vector.bn_stats(e_stats[s][:, j, :], hsrc[s][:, j * D:(j + 1) * D])
                last.then_inc(e_stats_done[s], 1)
                dve.wait_ge(e_stats_done[s], 1)
                row_variance(e_stats[s], e_mean[s][:, :], e_dif[s][:, :], e_var[s][:, :], e_var_done[s])
                dve.wait_ge(e_std_done[s], 1)
                row_scale(e_mean[s][:, :], e_rstd[s][:, :], e_shift[s][:, :], e_scale_done[s])
                rows = hsrc[s][:, :].rearrange("p (j d) -> p j d", d=D)
                scale_rows(rows, rows, e_rstd[s][:, :], e_shift[s][:, :], e_scaled[s])

            dve.wait_ge(consts, 5)
            dve.wait_ge(list_copied, LB)
            dve.wait_ge(bases_ready, 1)

            def choose_rows(g, s, rnd):
                dve.wait_ge(src_all_in[s], 16 * (rnd - (FR - 1)))
                nc.vector.tensor_scalar(src_off[:, :], src_all[s][:, :], row0[:, 0:1], None, ALU.subtract
                                        ).then_inc(src_off_ready, 1)
                dve.wait_ge(src_off_ready, g - (FG - 1))
                for b, (k0, k1) in enumerate(batches):
                    if not isinstance(g, int) or g > FG:
                        dve.wait_ge(fetched[b], g - FG)
                    nc.vector.tensor_tensor(
                        choose[:, k0:k1, :], src_off[:, :].unsqueeze(1).broadcast_to([P, k1 - k0, P]),
                        col_ids[:, k0:k1, :], ALU.is_equal).then_inc(chosen[b], 1)

            def group(g, s, rnd, last=False):
                if rnd is not FIRST:
                    dve.wait_ge(multiplied[s], rnd)
                nc.vector.tensor_tensor(
                    pick[s][:, :, :], node_id[:, :].unsqueeze(1).broadcast_to([P, EG, WIN]),
                    relT[:, bass.ds(g, 1), :].rearrange("p g j -> p (g j)").unsqueeze(2).broadcast_to([P, EG, WIN]),
                    ALU.is_equal).then_inc(picked[s], 1)
                fetches = not isinstance(g, int) or g >= FG
                if not last and (not isinstance(g, int) or g + 1 >= FG):
                    choose_rows(g + 1, (s + 1) % NS, rnd + (s + 1) // NS)
                if fetches:
                    dve.wait_ge(fetched[1], g - (FG - 1))
                    nc.vector.tensor_reduce(hsrc[s][:, PG * D:EG * D],
                                            row_ps[s % 2][:, 0:PARTS * D].rearrange("p (c d) -> p d c", c=PARTS),
                                            AX.X, ALU.add).then_inc(rows_summed, 1)
                    dve.wait_ge(rows_summed, g - (FG - 1))
                dve.wait_ge(attr_in[s], 32 * (rnd + 1))
                if rnd is FIRST:
                    row_moments(s)
                    dve.wait_ge(e_scaled[s], 1)
                    nc.vector.scalar_tensor_tensor(msg[s][:, :], hsrc[s][:, :], 0.0, msg[s][:, :], ALU.max, ALU.add
                                                   ).then_inc(summed[s], 1)
                elif last:
                    for n, (j0, j1) in enumerate(last_steps):
                        if n:
                            add_window(g - 1, s - 1, rnd)
                            dve.wait_ge(last_gathered, 16 * (PG - j0))
                        else:
                            dve.wait_ge(gathered[s], 16 * PG * (rnd - FR) + 16 * EG * FR + 16 * j1)
                        part = slice(j0 * D, j1 * D)
                        nc.vector.tensor_tensor(msg[s][:, part], msg[s][:, part], hsrc[s][:, part], ALU.add
                                                ).then_inc(summed[s], 1)
                    return
                else:
                    dve.wait_ge(gathered[s], 16 * PG * (rnd - (FR - 1)) + 16 * EG * FR)
                    nc.vector.tensor_tensor(msg[s][:, :], msg[s][:, :], hsrc[s][:, :], ALU.add).then_inc(summed[s], 1)
                if g is not FIRST:
                    add_window(g - 1, (s - 1) % NS, rnd if s > 0 else rnd - 1)

            def add_window(g, s, rnd):
                first = dve.value_load(bases[0:1, bass.ds(g, 1)], min_val=0, max_val=N - 1)
                dve.wait_ge(multiplied[s], rnd + 1)
                if s > 0:
                    dve.wait_ge(added[s - 1], rnd + 1)
                elif rnd is not FIRST:
                    dve.wait_ge(added[NS - 1], rnd)
                else:
                    dve.wait_ge(h_copied, hcopy_steps)
                nc.vector.tensor_tensor(sums[:, bass.ds(first, WIN)], sums[:, bass.ds(first, WIN)],
                                        win_ps[s % 2][0:D, 0:WIN], ALU.add).then_inc(added[s], 1)

            def rest_of_h(b):
                dve.wait_ge(wave_hi, b + 1)
                k0, k1 = batches[b]
                h = h_wave[:, 0:(k1 - k0) * D].rearrange("p (k d) -> p k d", d=D)
                nc.vector.tensor_tensor(h, h, table[:, k0:k1, 0, :], ALU.subtract).then_inc(wave_rest, 1)

            def low_part(b):
                dve.wait_ge(wave_mid, b + 1)
                k0, k1 = batches[b]
                h = h_wave[:, 0:(k1 - k0) * D].rearrange("p (k d) -> p k d", d=D)
                nc.vector.tensor_tensor(table[:, k0:k1, 2, :], h, table[:, k0:k1, 1, :], ALU.subtract
                                        ).then_inc(wave_lo, 1)

            for s in range(NS):
                group(s, s, FIRST)
            rest_of_h(0)
            nc.vector.tensor_scalar(t_pick[:, :], node_id[0:TE, :], tail_relT[:, 0:1], None, ALU.is_equal
                                    ).then_inc(t_picked, 1)
            dve.wait_ge(t_attr_in, 16)
            dve.wait_ge(t_gathered, 16)
            nc.vector.tensor_tensor(t_msg[:, :], t_msg[:, :], t_hsrc[:, :], ALU.add).then_inc(t_summed, 1)
            first = dve.value_load(bases[0:1, NG:NG + 1], min_val=0, max_val=N - 1)
            dve.wait_ge(t_multiplied, 1)
            dve.wait_ge(added[NS - 2], 1)
            nc.vector.tensor_tensor(sums[:, bass.ds(first, WIN)], sums[:, bass.ds(first, WIN)],
                                    y_ps[1][0:D, 0:WIN], ALU.add).then_inc(t_added, 1)
            dve.wait_ge(t_added, 1)

            def finish_block(j, k, nth):
                dve.wait_ge(y2_ready, nth)
                nc.vector.scalar_tensor_tensor(
                    hm[:, bass.ds(j, 1), :].rearrange("p j d -> p (j d)"), y_ps[k][:, 0:BC * D], 0.0,
                    xm[:, bass.ds(j, 1), :].rearrange("p j d -> p (j d)"), ALU.max, ALU.add).then_inc(out_ready, 1)

            def finish_tail(nth):
                dve.wait_ge(y2_ready, nth)
                nc.vector.scalar_tensor_tensor(out_t[0:NT, :], y_ps[NJ % 2][0:NT, 0:D], 0.0, xt[0:NT, :],
                                               ALU.max, ALU.add).then_inc(out_ready, 1)

            low_part(0)
            group(NS, 0, 1)
            group(NS + 1, 1, 1)
            rest_of_h(1)
            group(NS + 2, 2, 1)
            low_part(1)
            dve.wait_ge(col_ids_ready, 1)
            group(NS + 3, 3, 1)
            dve.wait_ge(chosen[1], 1)
            with dve.Fori(FR, LAG) as i:
                for s in range(NS):
                    group(i * NS + s, s, i)
            nc.vector.tensor_tensor(xm[:, :, :], xm[:, :, :], hm[:, :, :], ALU.add).then_inc(xh_done, 1)
            nc.vector.tensor_tensor(xt[0:NT, :], xt[0:NT, :], ht[0:NT, :], ALU.add).then_inc(xh_done, 1)
            dve.wait_ge(xh_done, 2)
            dve.wait_ge(h_stored, 48)
            with dve.Fori(LAG, ROUNDS) as i:
                for s in range(NS):
                    group(i * NS + s, s, i)
                finish_block(i - LAG, 0, i - (LAG - 1))
            for s in range(PEELED):
                group(ROUNDS * NS + s, s, ROUNDS, last=s == PEELED - 1)
            add_window(NG - 1, PEELED - 1, ROUNDS)
            dve.wait_ge(bases_ready, 1)
            is_outside = dve.value_load(outside[0:1, 0:1], min_val=0, max_val=1)
            is_redo = dve.value_load(redo[0:1, 0:1], min_val=0, max_val=1)
            for j in range(EARLY, NJ):
                finish_block(j, j % 2, j + 1)
            finish_tail(NJ + 1)

            with dve.If(is_outside == 1):
                nc.vector.tensor_scalar(far_row[:, :], rel_row[:, :], float(WIN), None, ALU.is_ge)
                nc.vector.tensor_scalar(tail_far[:, :], tail_rel[:, :], float(WIN), None, ALU.is_ge)
                nc.vector.tensor_scalar(dstf[:, :], dstf[:, :], 1.0, None, ALU.add)
                then(nc.vector.tensor_scalar(tail_dstf[:, :], tail_dstf[:, :], 1.0, None, ALU.add))
                nc.vector.tensor_tensor(far_row[:, :], far_row[:, :], dstf[:, :], ALU.mult)
                then(nc.vector.tensor_tensor(tail_far[:, :], tail_far[:, :], tail_dstf[:, :], ALU.mult))
                nc.vector.tensor_scalar(far_row[:, :], far_row[:, :], -1.0, None, ALU.add)
                nc.vector.tensor_scalar(tail_far[:, :], tail_far[:, :], -1.0, None, ALU.add
                                        ).then_inc(far_rows, 1)
                nc.vector.tensor_copy(block_id[:, :], node_id[:, :]).then_inc(f_block, 1)
                nc.vector.memset(eps[:, :], EPS).then_inc(f_added, 1)
                for k in range(LB):
                    dve.wait_ge(far_tr, k + 1)
                    nc.vector.tensor_copy(relT[:, :, k * LT:(k + 1) * LT],
                                          tr_ps[k % 2][:, 0:LT * NG].rearrange("p (j g) -> p g j", j=LT)
                                          ).then_inc(far_copied, 1)
                dve.wait_ge(far_tr, LB + 1)
                nc.vector.tensor_copy(tail_relT[:, :], y_ps[0][0:TE, 0:1]).then_inc(far_copied, 1)
                dve.wait_ge(far_copied, LB + 1)

                def restart(nth):
                    dve.wait_ge(f_block, (nth - 1) * (NB + 1) + 1)
                    nc.vector.tensor_copy(block_id[:, :], node_id[:, :]).then_inc(f_block, 1)

                def add_block(nth, w, whole):
                    dve.wait_ge(f_block, (nth - 1) * (NB + 1) + w + 2)
                    if whole:
                        nc.vector.tensor_tensor(
                            pick[0][:, :, :], block_id[:, :].unsqueeze(1).broadcast_to([P, EG, WIN]),
                            relT[:, bass.ds(nth - 1, 1), :].rearrange("p g j -> p (g j)").unsqueeze(2)
                            .broadcast_to([P, EG, WIN]), ALU.is_equal).then_inc(f_picked, 1)
                    else:
                        nc.vector.tensor_scalar(pick[0][0:TE, 0, :], block_id[0:TE, :], tail_relT[:, 0:1], None,
                                                ALU.is_equal).then_inc(f_picked, 1)
                    done = (nth - 1) * NB + w + 1
                    dve.wait_ge(f_picked, done)
                    nc.vector.tensor_scalar(block_id[:, :], block_id[:, :], float(WIN), None, ALU.add
                                            ).then_inc(f_block, 1)
                    dve.wait_ge(f_multiplied, done)
                    dve.wait_ge(f_added, done)
                    nc.vector.tensor_tensor(sums[:, bass.ds(w * WIN, WIN)], sums[:, bass.ds(w * WIN, WIN)],
                                            win_ps[0][0:D, 0:WIN], ALU.add).then_inc(f_added, 1)

                with dve.Fori(1, NG + 1) as nth:
                    dve.wait_ge(f_attr_in, 32 * nth)
                    dve.wait_ge(f_gathered, 16 * EG * nth)
                    nc.vector.tensor_tensor(msg[0][:, :], msg[0][:, :], hsrc[0][:, :], ALU.add).then_inc(f_summed, 1)
                    restart(nth)
                    with dve.Fori(0, NB) as w:
                        add_block(nth, w, True)
                dve.wait_ge(f_attr_in, 32 * NG + 16)
                dve.wait_ge(f_gathered, 16 * EG * NG + 16)
                nc.vector.tensor_tensor(msg[0][0:TE, 0:D], msg[0][0:TE, 0:D], hsrc[0][0:TE, 0:D], ALU.add
                                        ).then_inc(f_summed, 1)
                restart(NG + 1)
                with dve.Fori(0, NB) as w:
                    add_block(NG + 1, w, False)
                dve.wait_ge(f_added, (NG + 1) * NB + 1)

            with dve.If(is_redo == 1):
                dve.wait_ge(out_stored, 16 * (NJ + 1))
                nc.vector.memset(e_dif[0][:, :], 0.0).then_inc(sums_done, 1)
                with dve.Fori(0, NJ // 2) as q:
                    for k in range(2):
                        finish_block(q * 2 + k, k, q * 2 + (NJ + 2 + k))
                finish_tail(2 * NJ + 2)

        @block.tensor
        def _(pe):
            pe.wait_ge(consts, 5)
            pe.wait_ge(rows_ready, 1)
            def tile_of(v, j):
                return v[:, GPE:GE] if j == PG else v[:, 0:GPE].rearrange("g (p j) -> g j p", j=PG)[:, j, :]

            for k in range(LB):
                for t in range(LT):
                    last = nc.tensor.transpose(tr_ps[k % 2][:, t * NG:(t + 1) * NG], tile_of(rel_row, k * LT + t),
                                               ident[0:NG, 0:NG])
                last.then_inc(list_tr, 1)
            nc.tensor.transpose(y_ps[0][0:1, 0:NG], base[:, 0:1], ident[0:NG, 0:NG])
            nc.tensor.transpose(y_ps[0][0:1, P:P + NG], span[:, 0:1], ident[0:NG, 0:NG])
            nc.tensor.transpose(y_ps[0][0:TE, 2 * P:2 * P + 1], tail_rel[:, :], ident[0:1, 0:1]
                                ).then_inc(bases_tr, 1)

            def window(s, rnd, steps=((0, EG),)):
                pe.wait_ge(picked[s], rnd + 1)
                if s >= 2:
                    pe.wait_ge(added[s - 2], rnd + 1)
                elif rnd is not FIRST:
                    pe.wait_ge(added[s - 2], rnd)
                for n, (j0, j1) in enumerate(steps):
                    pe.wait_ge(relu_done[s], rnd + 1 + n)
                    for j in range(j0, j1):
                        last = nc.tensor.matmul(win_ps[s % 2][0:D, 0:WIN], msg[s][:, j * D:(j + 1) * D],
                                                pick[s][:, j, :], start=(j == 0), stop=(j == EG - 1))
                last.then_inc(multiplied[s], 1)

            pe.wait_ge(list_copied, LB)
            for j in range(NJ):
                pe.wait_ge(h_done, 1 + j // (NJ // 2))
                if j >= 2:
                    pe.wait_ge(h_copied, j - 1)
                for t in range(BC):
                    last = nc.tensor.transpose(tr_ps[j % 2][0:D, t * P:(t + 1) * P], hm[:, j, t * D:(t + 1) * D],
                                               ident[:, :])
                last.then_inc(h_tr, 1)
                if j == NJ // 2:
                    window(0, FIRST)
            pe.wait_ge(h_copied, NJ - 1)
            nc.tensor.transpose(tr_ps[NJ % 2][0:D, 0:NT], ht[0:NT, :], ident[0:NT, 0:NT]).then_inc(h_tr, 1)

            for s in range(1, NS):
                window(s, FIRST)
            def fetch_rows(g, s):
                if not isinstance(g, int) or g > FG + 1:
                    pe.wait_ge(rows_summed, g - (FG + 1))
                for b, (k0, k1) in enumerate(batches):
                    pe.wait_ge(chosen[b], g - (FG - 1))
                    for k in range(k0, k1):
                        last = nc.tensor.matmul(row_ps[s % 2][:, 0:PARTS * D], choose[:, k, :],
                                                table[:, k, :, :].rearrange("p c d -> p (c d)"),
                                                start=(k == 0), stop=(k == TK - 1))
                    last.then_inc(fetched[b], 1)

            def step(g, s, rnd):
                if not isinstance(g, int) or g + 1 >= FG:
                    fetch_rows(g + 1, (s + 1) % NS)
                window(s, rnd)

            pe.wait_ge(t_picked, 1)
            pe.wait_ge(t_relu, 1)
            nc.tensor.matmul(y_ps[1][0:D, 0:WIN], t_msg[:, :], t_pick[:, :], start=True, stop=True
                             ).then_inc(t_multiplied, 1)

            blocks = sums[:, 0:NM].rearrange("f (j p t) -> f j t p", p=P, t=BC)

            def layer1(j, k):
                nc.tensor.matmul(tr_ps[k][0:D, 0:BN], w1[:, :],
                                 blocks[:, bass.ds(j, 1), :, :].rearrange("f j t p -> f (j t) p"),
                                 start=True, stop=True).then_inc(y1_ready, 1)

            def layer2(k, nth):
                pe.wait_ge(act1_ready, nth)
                for t in range(BC):
                    last = nc.tensor.matmul(y_ps[k][:, t * D:(t + 1) * D], act1[k][:, t * P:(t + 1) * P],
                                            w2b[:, :], start=True, stop=True)
                last.then_inc(y2_ready, 1)

            def tail_layers(nth):
                k = NJ % 2
                nc.tensor.matmul(tr_ps[k][0:D, 0:NT], w1[:, :], sums[:, NM:N], start=True, stop=True
                                 ).then_inc(y1_ready, 1)
                pe.wait_ge(act1_ready, nth)
                nc.tensor.matmul(y_ps[k][0:NT, 0:D], act1[k][:, 0:NT], w2b[:, :], start=True, stop=True
                                 ).then_inc(y2_ready, 1)

            for s in range(NS):
                if s == NS - 1:
                    pe.wait_ge(wave_lo, 2)
                step(NS + s, s, 1)
            with pe.Fori(FR, LAG) as i:
                for s in range(NS):
                    step(i * NS + s, s, i)
            pe.wait_ge(weights_in, 64)
            with pe.Fori(LAG, ROUNDS) as i:
                for s in range(NS):
                    fetch_rows(i * NS + s + 1, (s + 1) % NS)
                    if s == FB:
                        pe.wait_ge(added[FB - 1], i + 1)
                        layer1(i - LAG, 0)
                    if s == FB + 1:
                        layer2(0, i - (LAG - 1))
                    window(s, i)
            for s in range(PEELED - 1):
                step(ROUNDS * NS + s, s, ROUNDS)
            window(PEELED - 1, ROUNDS, last_steps)
            pe.wait_ge(bases_ready, 1)
            is_outside = pe.value_load(outside[0:1, 0:1], min_val=0, max_val=1)
            is_redo = pe.value_load(redo[0:1, 0:1], min_val=0, max_val=1)
            pe.wait_ge(added[PEELED - 1], ROUNDS + 1)
            for j in range(EARLY, NJ):
                layer1(j, j % 2)
            for j in range(EARLY, NJ):
                layer2(j % 2, j + 1)
            pe.wait_ge(out_ready, NJ - 1)
            tail_layers(NJ + 1)

            with pe.If(is_outside == 1):
                pe.wait_ge(far_rows, 1)
                for k in range(LB):
                    for t in range(LT):
                        last = nc.tensor.transpose(tr_ps[k % 2][:, t * NG:(t + 1) * NG], tile_of(far_row, k * LT + t),
                                                   ident[0:NG, 0:NG])
                    last.then_inc(far_tr, 1)
                nc.tensor.transpose(y_ps[0][0:TE, 0:1], tail_far[:, :], ident[0:1, 0:1]).then_inc(far_tr, 1)
                pe.wait_ge(far_copied, LB + 1)
                with pe.Fori(1, NG + 1) as nth:
                    pe.wait_ge(far_rows, 1)
                    pe.wait_ge(f_relu, nth)
                    with pe.Fori(0, NB) as w:
                        pe.wait_ge(f_picked, (nth - 1) * NB + w + 1)
                        pe.wait_ge(f_added, (nth - 1) * NB + w + 1)
                        for j in range(EG):
                            last = nc.tensor.matmul(win_ps[0][0:D, 0:WIN], msg[0][:, j * D:(j + 1) * D],
                                                    pick[0][:, j, :], start=(j == 0), stop=(j == EG - 1))
                        last.then_inc(f_multiplied, 1)
                pe.wait_ge(f_relu, NG + 1)
                with pe.Fori(0, NB) as w:
                    pe.wait_ge(f_picked, NG * NB + w + 1)
                    pe.wait_ge(f_added, NG * NB + w + 1)
                    nc.tensor.matmul(win_ps[0][0:D, 0:WIN], msg[0][0:TE, 0:D], pick[0][0:TE, 0, :],
                                     start=True, stop=True).then_inc(f_multiplied, 1)

            with pe.If(is_redo == 1):
                pe.wait_ge(sums_done, 1)
                with pe.Fori(0, NJ // 2) as q:
                    for k in range(2):
                        layer1(q * 2 + k, k)
                    pe.wait_ge(out_ready, q * 2 + (NJ + 1))
                    for k in range(2):
                        layer2(k, q * 2 + (NJ + 2 + k))
                pe.wait_ge(out_ready, 2 * NJ + 1)
                tail_layers(2 * NJ + 2)


_INS = ["x", "src", "dst", "edge_attr_96", "L0_gnn_W1", "L0_gnn_b1", "L0_gnn_W2", "L0_gnn_b2"]


def kernel(**inputs):
    import numpy as _np
    import concourse.bacc as _bacc
    from concourse.bass_utils import run_bass_kernel_spmd as _run

    nc = _bacc.Bacc("TRN2", target_bir_lowering=False, num_devices=1)
    arrays, args = {}, []
    for name in _INS:
        a = _np.ascontiguousarray(inputs[name])
        arrays[name] = a
        args.append(nc.dram_tensor(name, a.shape, mybir.dt.from_np(a.dtype), kind="ExternalInput").ap())
    args.append(nc.dram_tensor("out", arrays["x"].shape, F32, kind="ExternalOutput").ap())
    gnn_kernel(nc, *args)
    r = _run(nc, [arrays], core_ids=[0])
    return r.results[0]["out"]
```
